# Optimizing a Trainium2 kernel written in Bass

```python
import numpy as np
import jax
import jax.numpy as jnp

def _softmax(x, axis=-1):
    return jax.nn.softmax(x, axis=axis)

def _gelu(x):
    return jax.nn.gelu(x, approximate=True)

def _silu(x):
    return jax.nn.silu(x)

def _sigmoid(x):
    return jax.nn.sigmoid(x)

def _layernorm(x, axis=-1, eps=1e-05):
    m = jnp.mean(x, axis=axis, keepdims=True)
    v = jnp.var(x, axis=axis, keepdims=True)
    return (x - m) / jnp.sqrt(v + eps)

def _scatter_add(tgt, idx, src, axis=0):
    return tgt.at[idx].add(src)

def _segment_sum(src, seg, n):
    return jax.ops.segment_sum(src, seg, n)
kernel_name = 'mk_gnn_resnorm_d4_gnn_r64_ac9b98'

def setup_inputs(seed: int=0):
    np.random.seed(seed)
    _w = jnp.asarray

    def _rec_inputs():
        import jax
        import jax.numpy as jnp
        _gk = jax.random.key(seed)
        x = -0.0003713 + 1 * jax.random.normal(jax.random.fold_in(_gk, 1), (100000, 128), jnp.float32)
        src = jax.random.randint(jax.random.fold_in(_gk, 2), (25000,), 0, 100000, jnp.int32)
        dst = jax.random.randint(jax.random.fold_in(_gk, 3), (25000,), 0, 100000, jnp.int32)
        _o = jnp.argsort(dst, stable=True)
        src = src[_o]
        dst = dst[_o]
        edge_type_9 = jax.random.randint(jax.random.fold_in(_gk, 13), (25000,), 0, 9, jnp.int32)
        return (x, src, dst, edge_type_9)
    x, src, dst, edge_type_9 = _rec_inputs()

    def _L0_gnn_setup():
        import jax, jax.numpy as jnp
        import numpy as np
        N_NODES = 100000
        N_EDGES = 25000
        HIDDEN = 128

        def _layernorm(x, gamma, beta, eps=1e-05):
            mu = jnp.mean(x, axis=-1, keepdims=True)
            var = jnp.mean(jnp.square(x - mu), axis=-1, keepdims=True)
            return (x - mu) * jax.lax.rsqrt(var + eps) * gamma + beta
        key = jax.random.key(seed)
        k1, k2, k3, k4 = jax.random.split(key, 4)
        h = jax.random.normal(k1, (N_NODES, HIDDEN), dtype=jnp.float32)
        edge_src = jax.random.randint(k2, (N_EDGES,), 0, N_NODES, dtype=jnp.int32)
        edge_dst = jax.random.randint(k3, (N_EDGES,), 0, N_NODES, dtype=jnp.int32)
        bound = 1.0 / np.sqrt(HIDDEN)
        W = jax.random.uniform(k4, (HIDDEN, HIDDEN), dtype=jnp.float32, minval=-bound, maxval=bound)
        gamma = jnp.ones((HIDDEN,), dtype=jnp.float32)
        beta = jnp.zeros((HIDDEN,), dtype=jnp.float32)
        return {'h': h, 'edge_src': edge_src, 'edge_dst': edge_dst, 'W': W, 'gamma': gamma, 'beta': beta}
    _L0_gnn_all = _L0_gnn_setup()
    _L0_gnn_in = {k: v for k, v in _L0_gnn_all.items() if k in ('W', 'gamma', 'beta')}
    del _L0_gnn_all

    def _L1_gnn_setup():
        import jax, jax.numpy as jnp
        import numpy as np
        N_NODES = 100000
        N_EDGES = 25000
        D_IN = 128
        D_OUT = 128
        NEG_SLOPE = 0.01
        key = jax.random.key(seed)
        k1, k2, k3, k4, k5 = jax.random.split(key, 5)
        h = jax.random.normal(k1, (N_NODES, D_IN), dtype=jnp.float32)
        W = jax.random.normal(k2, (D_IN, D_OUT), dtype=jnp.float32) / np.sqrt(D_IN)
        attn_w = jax.random.normal(k3, (2 * D_OUT,), dtype=jnp.float32) / np.sqrt(2 * D_OUT)
        edge_src = jax.random.randint(k4, (N_EDGES,), 0, N_NODES, dtype=jnp.int32)
        edge_dst = jax.random.randint(k5, (N_EDGES,), 0, N_NODES, dtype=jnp.int32)
        return {'h': h, 'W': W, 'attn_w': attn_w, 'edge_src': edge_src, 'edge_dst': edge_dst}
    _L1_gnn_all = _L1_gnn_setup()
    _L1_gnn_in = {k: v for k, v in _L1_gnn_all.items() if k in ('W', 'attn_w')}
    del _L1_gnn_all

    def _L2_gnn_setup():
        import jax, jax.numpy as jnp
        import numpy as np
        N_NODES = 100000
        N_EDGES = 10000
        D_IN = 128
        D_OUT = 128
        EPS = 1e-05
        key = jax.random.key(seed)
        k_h, k_src, k_dst, k_ws, k_wn = jax.random.split(key, 5)
        h = jax.random.normal(k_h, (N_NODES, D_IN), dtype=jnp.float32)
        src = jax.random.randint(k_src, (N_EDGES,), 0, N_NODES, dtype=jnp.int32)
        dst = jax.random.randint(k_dst, (N_EDGES,), 0, N_NODES, dtype=jnp.int32)
        gamma = jnp.ones((D_IN,), dtype=jnp.float32)
        beta = jnp.zeros((D_IN,), dtype=jnp.float32)
        scale = 1.0 / np.sqrt(D_IN)
        W_self = jax.random.normal(k_ws, (D_IN, D_OUT), dtype=jnp.float32) * scale
        W_neigh = jax.random.normal(k_wn, (D_IN, D_OUT), dtype=jnp.float32) * scale
        b = jnp.zeros((D_OUT,), dtype=jnp.float32)
        return {'h': h, 'src': src, 'dst': dst, 'gamma': gamma, 'beta': beta, 'W_self': W_self, 'W_neigh': W_neigh, 'b': b}
    _L2_gnn_all = _L2_gnn_setup()
    _L2_gnn_in = {k: v for k, v in _L2_gnn_all.items() if k in ('gamma', 'beta', 'W_self', 'W_neigh', 'b')}
    del _L2_gnn_all

    def _L3_gnn_setup():
        import jax, jax.numpy as jnp
        import numpy as np
        NUM_EDGE_TYPES = 8
        HIDDEN = 128
        N_NODES = 50000
        N_EDGES = 9375

        def _gru_cell(x, h, W_ih, W_hh, b_ih, b_hh):
            H = h.shape[-1]
            gi = x @ W_ih.T + b_ih
            gh = h @ W_hh.T + b_hh
            i_r, i_z, i_n = (gi[:, :H], gi[:, H:2 * H], gi[:, 2 * H:])
            h_r, h_z, h_n = (gh[:, :H], gh[:, H:2 * H], gh[:, 2 * H:])
            r = jax.nn.sigmoid(i_r + h_r)
            z = jax.nn.sigmoid(i_z + h_z)
            n = jnp.tanh(i_n + r * h_n)
            return (1.0 - z) * n + z * h
        key = jax.random.key(seed)
        ks = jax.random.split(key, 10)
        H = HIDDEN
        h = jax.random.normal(ks[0], (N_NODES, H), dtype=jnp.float32)
        edge_index = jax.random.randint(ks[1], (2, N_EDGES), 0, N_NODES, dtype=jnp.int32)
        edge_type = jax.random.randint(ks[2], (N_EDGES,), 0, NUM_EDGE_TYPES + 1, dtype=jnp.int32)
        s = 1.0 / np.sqrt(H)
        W_msg = jax.random.uniform(ks[3], (H, H), jnp.float32, -s, s)
        b_msg = jax.random.uniform(ks[4], (H,), jnp.float32, -s, s)
        edge_embed = jax.random.normal(ks[5], (NUM_EDGE_TYPES + 1, H), dtype=jnp.float32)
        W_ih = jax.random.uniform(ks[6], (3 * H, H), jnp.float32, -s, s)
        W_hh = jax.random.uniform(ks[7], (3 * H, H), jnp.float32, -s, s)
        b_ih = jax.random.uniform(ks[8], (3 * H,), jnp.float32, -s, s)
        b_hh = jax.random.uniform(ks[9], (3 * H,), jnp.float32, -s, s)
        return {'h': h, 'edge_index': edge_index, 'edge_type': edge_type, 'num_nodes': N_NODES, 'W_msg': W_msg, 'b_msg': b_msg, 'edge_embed': edge_embed, 'W_ih': W_ih, 'W_hh': W_hh, 'b_ih': b_ih, 'b_hh': b_hh}
    _L3_gnn_all = _L3_gnn_setup()
    _L3_gnn_in = {k: v for k, v in _L3_gnn_all.items() if k in ('W_msg', 'b_msg', 'edge_embed', 'W_ih', 'W_hh', 'b_ih', 'b_hh')}
    del _L3_gnn_all
    return {'x': x, 'src': src, 'dst': dst, 'edge_type_9': edge_type_9, 'L0_gnn_W': _L0_gnn_in['W'], 'L0_gnn_gamma': _L0_gnn_in['gamma'], 'L0_gnn_beta': _L0_gnn_in['beta'], 'L1_gnn_W': _L1_gnn_in['W'], 'L1_gnn_attn_w': _L1_gnn_in['attn_w'], 'L2_gnn_gamma': _L2_gnn_in['gamma'], 'L2_gnn_beta': _L2_gnn_in['beta'], 'L2_gnn_W_self': _L2_gnn_in['W_self'], 'L2_gnn_W_neigh': _L2_gnn_in['W_neigh'], 'L2_gnn_b': _L2_gnn_in['b'], 'L3_gnn_W_msg': _L3_gnn_in['W_msg'], 'L3_gnn_b_msg': _L3_gnn_in['b_msg'], 'L3_gnn_edge_embed': _L3_gnn_in['edge_embed'], 'L3_gnn_W_ih': _L3_gnn_in['W_ih'], 'L3_gnn_W_hh': _L3_gnn_in['W_hh'], 'L3_gnn_b_ih': _L3_gnn_in['b_ih'], 'L3_gnn_b_hh': _L3_gnn_in['b_hh']}

def reference(x, src, dst, edge_type_9, L0_gnn_W, L0_gnn_gamma, L0_gnn_beta, L1_gnn_W, L1_gnn_attn_w, L2_gnn_gamma, L2_gnn_beta, L2_gnn_W_self, L2_gnn_W_neigh, L2_gnn_b, L3_gnn_W_msg, L3_gnn_b_msg, L3_gnn_edge_embed, L3_gnn_W_ih, L3_gnn_W_hh, L3_gnn_b_ih, L3_gnn_b_hh):
    import jax
    import jax.numpy as jnp

    def _L0_gnn_ref(h, edge_src, edge_dst, W, gamma, beta):
        import jax, jax.numpy as jnp
        import numpy as np
        N_NODES = 100000
        N_EDGES = 25000
        HIDDEN = 128

        def _layernorm(x, gamma, beta, eps=1e-05):
            mu = jnp.mean(x, axis=-1, keepdims=True)
            var = jnp.mean(jnp.square(x - mu), axis=-1, keepdims=True)
            return (x - mu) * jax.lax.rsqrt(var + eps) * gamma + beta
        msgs = h[edge_src]
        u = jax.ops.segment_sum(msgs, edge_dst, num_segments=N_NODES)
        h1 = jax.nn.relu(u @ W.T) + h
        return _layernorm(h1, gamma, beta)

    def _L1_gnn_ref(h, W, attn_w, edge_src, edge_dst):
        import jax, jax.numpy as jnp
        import numpy as np
        N_NODES = 100000
        N_EDGES = 25000
        D_IN = 128
        D_OUT = 128
        NEG_SLOPE = 0.01
        n = h.shape[0]
        d = W.shape[1]
        z = h @ W
        s_src = z @ attn_w[:d]
        s_dst = z @ attn_w[d:]
        e = jax.nn.leaky_relu(s_src[edge_src] + s_dst[edge_dst], NEG_SLOPE)
        m = jax.ops.segment_max(e, edge_dst, num_segments=n)
        ex = jnp.exp(e - m[edge_dst])
        denom = jax.ops.segment_sum(ex, edge_dst, num_segments=n)
        alpha = ex / denom[edge_dst]
        out = jax.ops.segment_sum(alpha[:, None] * z[edge_src], edge_dst, num_segments=n)
        return out

    def _L2_gnn_ref(h, src, dst, gamma, beta, W_self, W_neigh, b):
        import jax, jax.numpy as jnp
        import numpy as np
        N_NODES = 100000
        N_EDGES = 10000
        D_IN = 128
        D_OUT = 128
        EPS = 1e-05
        mu = jnp.mean(h, axis=-1, keepdims=True)
        var = jnp.mean(jnp.square(h - mu), axis=-1, keepdims=True)
        hn = (h - mu) * jax.lax.rsqrt(var + EPS) * gamma + beta
        n = h.shape[0]
        msg_sum = jax.ops.segment_sum(hn[src], dst, num_segments=n)
        deg = jax.ops.segment_sum(jnp.ones_like(dst, dtype=hn.dtype), dst, num_segments=n)
        h_neigh = msg_sum / jnp.maximum(deg, 1.0)[:, None]
        out = hn @ W_self + h_neigh @ W_neigh + b
        return out

    def _L3_gnn_ref(h, edge_index, edge_type, num_nodes, W_msg, b_msg, edge_embed, W_ih, W_hh, b_ih, b_hh):
        import jax, jax.numpy as jnp
        import numpy as np
        NUM_EDGE_TYPES = 8
        HIDDEN = 128
        N_NODES = 50000
        N_EDGES = 9375

        def _gru_cell(x, h, W_ih, W_hh, b_ih, b_hh):
            H = h.shape[-1]
            gi = x @ W_ih.T + b_ih
            gh = h @ W_hh.T + b_hh
            i_r, i_z, i_n = (gi[:, :H], gi[:, H:2 * H], gi[:, 2 * H:])
            h_r, h_z, h_n = (gh[:, :H], gh[:, H:2 * H], gh[:, 2 * H:])
            r = jax.nn.sigmoid(i_r + h_r)
            z = jax.nn.sigmoid(i_z + h_z)
            n = jnp.tanh(i_n + r * h_n)
            return (1.0 - z) * n + z * h
        src = edge_index[0]
        dst = edge_index[1]
        src_h = h[src] @ W_msg.T + b_msg
        emb = edge_embed[jnp.clip(edge_type, 0, NUM_EDGE_TYPES)]
        msg = src_h + emb
        messages = jax.ops.segment_sum(msg, dst, num_segments=num_nodes)
        h_new = _gru_cell(messages, h[:num_nodes], W_ih, W_hh, b_ih, b_hh)
        result = jnp.zeros_like(h).at[:num_nodes].set(h_new)
        return result
    edge_index = jnp.stack([src, dst])
    x = _layernorm(x + _L0_gnn_ref(x, src, dst, L0_gnn_W, L0_gnn_gamma, L0_gnn_beta), axis=-1)
    x = _layernorm(x + _L1_gnn_ref(x, L1_gnn_W, L1_gnn_attn_w, src, dst), axis=-1)
    x = _layernorm(x + _L2_gnn_ref(x, src, dst, L2_gnn_gamma, L2_gnn_beta, L2_gnn_W_self, L2_gnn_W_neigh, L2_gnn_b), axis=-1)
    x = _layernorm(x + _L3_gnn_ref(x, edge_index, edge_type_9, 100000, L3_gnn_W_msg, L3_gnn_b_msg, L3_gnn_edge_embed, L3_gnn_W_ih, L3_gnn_W_hh, L3_gnn_b_ih, L3_gnn_b_hh), axis=-1)
    return x

_drawn_inputs = setup_inputs


def setup_inputs(seed=0):
    import zlib

    import numpy as np

    out = dict(_drawn_inputs(seed))
    spreads = {'L0_gnn_gamma': (1.0, 0.2),
     'L0_gnn_beta': (0.0, 0.1),
     'L2_gnn_gamma': (1.0, 0.2),
     'L2_gnn_beta': (0.0, 0.1),
     'L2_gnn_b': (0.0, 0.1)}
    factors = {'L3_gnn_b_msg': 8.0, 'L3_gnn_b_ih': 3.098, 'L3_gnn_b_hh': 4.877}
    for name, (base, spread) in spreads.items():
        noise = np.random.default_rng([zlib.crc32(name.encode()), seed]).standard_normal(out[name].shape)
        drawn = base * np.exp(spread * noise) if base else spread * noise
        out[name] = jnp.asarray(drawn.astype(out[name].dtype))
    for name, factor in factors.items():
        out[name] = (out[name] * factor).astype(out[name].dtype)
    return out
```

```python
from contextlib import ExitStack

import concourse.bass as bass
from concourse import mybir

F32 = mybir.dt.float32
I32 = mybir.dt.int32
ALU = mybir.AluOpType
ACT = mybir.ActivationFunctionType
AX = mybir.AxisListType.X
DS = bass.ds

P = 128
D = 128
EPS = 1e-5
SLOPE = 0.01
NEG = 1e30
MAGIC = 1597463007.0
TYPES = 9
CNT = TYPES + 1
R = 4


class Phase:

    def __init__(self, steps, stages, rings, st, rg, base):
        self.steps, self.st, self.rg = steps, st, rg
        self.mult, self.dmas = dict(stages), dict(rings)
        self.base = {k: base.get(k, 0) for k in list(self.mult) + [(k, r) for k in self.dmas for r in range(R)]}
        for k, m in self.mult.items():
            base[k] = base.get(k, 0) + m * steps
        for k, m in self.dmas.items():
            for r in range(R):
                base[(k, r)] = base.get((k, r), 0) + 16 * m * len(range(r, steps, R))
        self.end = {k: base[k] for k in self.base}

    def done(self, name, g, k=None):
        m = self.mult[name]
        return self.st[name], g * m + (self.base[name] + (m if k is None else k))

    def moved(self, name, g, r):
        m = self.dmas[name]
        return self.rg[name][r], (g - r) * (16 * m // R) + (self.base[(name, r)] + 16 * m)

    def old(self, g, n=R):
        return not isinstance(g, int) or g >= n


class Steps:

    def __init__(self, sem, names):
        self.sem, self.names, self.k = sem, names.split(), 0

    def did(self, ins, name):
        assert self.names[self.k] == name, (self.names[self.k], name)
        self.k += 1
        ins.then_inc(self.sem, 1)

    def at(self, name):
        return self.sem, self.names.index(name) + 1


def pipeline(eng, steps, stages):
    lag = max(o for o, _ in stages)
    lo, hi = -(-(lag + R) // R) * R, steps // R * R
    for i in range(lo):
        for o, body in stages:
            if 0 <= i - o < steps:
                body(i - o, (i - o) % R)
    if hi > lo:
        with eng.Fori(lo // R, hi // R) as block:
            for k in range(R):
                for o, body in stages:
                    body(block * R + (k - o), (k - o) % R)
    for i in range(max(hi, lo), steps + lag):
        for o, body in stages:
            if 0 <= i - o < steps:
                body(i - o, (i - o) % R)


def gnn_program(nc, x, src, dst, etype, w0, gamma0, beta0, w1, attn, gamma2, beta2, w_self, w_neigh, b2,
                w_msg, b_msg, embed, w_ih, w_hh, b_ih, b_hh, out):
    N, E = x.shape[0], src.shape[0]
    T = -(-E // (8 * P)) * 8
    HT = T // 2
    NS = P * T
    BIG = 1 << 20
    W = 8
    BLK = W * P
    ND = -(-N // BLK)
    TAILP = (N - (ND - 1) * BLK) // W
    assert TAILP * W == N - (ND - 1) * BLK and T == 200
    C1N = ND // 2
    GS = T // 4

    ctx = ExitStack()
    with ctx:
        def sb(name, shape, dt=F32):
            return ctx.enter_context(nc.sbuf_tensor(name, shape, dt))

        def sem(name):
            return ctx.enter_context(nc.semaphore(name))

        tab = [x] + [nc.dram_tensor(f"t{k}", [N, D], F32) for k in (1, 2, 3)]
        xs = [nc.dram_tensor(f"xs{k}", [NS, D], F32) for k in range(4)]
        agg_d = nc.dram_tensor("agg_d", [NS, D], F32)
        cnt_d = nc.dram_tensor("cnt_d", [NS, CNT], F32)
        dst_d = nc.dram_tensor("dst_d", [NS], F32)
        seq_d = nc.dram_tensor("seq_d", [NS], F32)
        seq2_d = nc.dram_tensor("seq2_d", [NS], F32)
        row_d = nc.dram_tensor("row_d", [P], F32)
        row2_d = nc.dram_tensor("row2_d", [P], F32)

        def slots(t):
            return t.rearrange("(p t) d -> p t d", p=P)

        def nodes(t, g):
            if isinstance(g, int):
                return t[g * BLK:min(N, (g + 1) * BLK), :].rearrange("(p t) d -> p t d", t=W)
            return t[DS(g * BLK, BLK), :].rearrange("(p t) d -> p t d", t=W)

        def tiles(t, g, n):
            if isinstance(g, int):
                return t[:, g * n:(g + 1) * n]
            return t[:, DS(g * n, n)]

        S = sb("S", [P, T, D])
        BUF = sb("BUF", [P, 144, D])
        gring = sb("gring", [P, R, 4, D])
        iring = sb("iring", [P, R, 4], I32)
        oring = sb("oring", [P, R, 8], I32)
        srci, dgi, sci = sb("srci", [P, T], I32), sb("dgi", [P, T], I32), sb("sci", [P, T], I32)
        dstc = sb("dstc", [P, T])
        dprev = sb("dprev", [P, T])
        lastc = sb("lastc", [P, T])
        typec = sb("typec", [P, T])
        rdeg, sS, sD, ew, mx = sb("rdeg", [P, T]), sb("sS", [P, T]), sb("sD", [P, T]), sb("ew", [P, T]), sb("mx", [P, T])
        col = sb("col", [P, 32])
        row = sb("row", [1, 8, P])
        ident, onesf, cen = sb("ident", [P, P]), sb("onesf", [P, P]), sb("cen", [P, P])
        e127 = sb("e127", [P, 1])
        gam_b = sb("gam_b", [P, D])
        wa_b = sb("wa_b", [P, 2, D])
        bias_r = sb("bias_r", [1, 3, D])
        w0T, w1s, wsc, wnc = sb("w0T", [P, D]), sb("w1s", [P, D]), sb("wsc", [P, D]), sb("wnc", [P, D])
        whT, wcT = sb("whT", [P, 3 * D]), sb("wcT", [P, 3 * D])
        wcE = sb("wcE", [TYPES, 3 * D])
        st1, st2 = sb("st1", [P, W, 6]), sb("st2", [P, W, 6])
        mv1, mv2 = sb("mv1", [P, R, W, 2]), sb("mv2", [P, R, W, 2])
        sd1, sd2, sd3 = sb("sd1", [P, R, W]), sb("sd2", [P, R, W]), sb("sd3", [P, R, W])
        rs1, rs2, rs3 = sb("rs1", [P, R, W]), sb("rs2", [P, R, W]), sb("rs3", [P, R, W])
        nm1, nm2 = sb("nm1", [P, R, W]), sb("nm2", [P, R, W])
        nwt, nwi = sb("nwt", [P, 2, W]), sb("nwi", [P, W], I32)
        epsc = sb("epsc", [P, 1])

        PS = ctx.enter_context(nc.psum_tensor("PS", [P, 8, 512], F32))

        def bank(b, n=1):
            return PS[:, b:b + n, :]

        def wide(b):
            return PS[:, b:b + 2, :].rearrange("p b (t d) -> p (b t) d", d=D)

        def ring(first, r, w=W):
            return BUF[:, first + r * w:first + (r + 1) * w, :]

        def flat(t):
            return t.rearrange("p a b -> p (a b)")

        def c(k, n=1):
            return col[:, k:k + n]

        G2, B2, BM, A1, A2, BIH, BHH, BR, BZ, CC, TM = 0, 1, 2, 3, 4, 5, 8, 11, 12, 13, 14

        st = {k: sem("s_" + k) for k in (
            "bn1 ag1 sq1 rc1 nm1 xn gm y bn2 ag2 sq2 rc2 nm2 apd apa tr ev h mm rel q r3 sq3 u tg eg tc ec "
            "g0 g1 sg0 sg1 th ot tn w nw ix so mk sm cv qq sdp").split()}
        rg = {k: [sem(f"{k}{r}") for r in range(R)] for k in "ldx ldg ldc sto st2 gat plc sct".split()}
        loaded, bounce = sem("loaded"), sem("bounce")
        pool_pass = sem("pool_pass")
        V = Steps(sem("dve_steps"),
                  "idf idx cen embc wcx oh sDv seqv e seqe exa rv")
        PEQ = Steps(sem("pe_steps"), "ids emb wcx sdv sdb ev mb")
        ACQ = Steps(sem("act_steps"), "exp rv")
        POOL = Steps(sem("pool_steps"), "consts ident")
        SEQ = Steps(sem("scan_steps"), "a0 a2 a5 b0 b2 c0 c2 c5")
        SPQ = sem("sp_steps")

        base = {}

        def phase(steps, stages, rings):
            return Phase(steps, [(s.split(":")[0], int((s.split(":") + ["1"])[1])) for s in stages.split()],
                         [(s.split(":")[0], int((s.split(":") + ["1"])[1])) for s in rings.split()], st, rg, base)

        GATHER, SUM = "gat:4 plc", "mk sm:4 cv:4"
        LN1, LN2 = "bn1 ag1 sq1 rc1 nm1", "bn2 ag2 sq2 rc2 nm2 apd apa"
        CS = "tr ev g0 g1 sg0 sg1 th ot tn:2 w:3 y bn2 ag2 nw:13 apa"
        ph = {}
        ph["G0"] = phase(GS, "ix", GATHER)
        ph["GD"] = phase(GS, "ix", GATHER)
        ph["A"] = phase(ND, LN1 + " xn gm y " + LN2, "ldx sto")
        ph["S0"] = phase(GS, SUM + " qq", "ldg sto:2")
        ph["L0"] = phase(T // W, LN1 + " xn gm y " + LN2 + " tr ev h rel sdp:2 so", "ldx ldg sto sct:8")
        ph["G1"] = phase(GS, "ix", GATHER)
        ph["B"] = phase(ND, LN1 + " xn q:2 sq3 r3 u tr ev y " + LN2, "ldx sto st2")
        ph["S1"] = phase(GS, SUM + " qq:3", "ldg sto")
        ph["L1"] = phase(T // W, "tr ev y so " + LN2, "ldx ldg sto sct:8")
        ph["G2"] = phase(GS, "ix", GATHER)
        ph["C1"] = phase(C1N, CS, "ldx sto")
        ph["S2"] = phase(GS, SUM + " qq", "ldg sto")
        ph["L2"] = phase(T // W, LN1 + " u tr ev tg eg y so " + LN2, "ldx ldg sto sct:8")
        ph["G3"] = phase(GS, "ix", GATHER)
        ph["C2"] = phase(ND - C1N, CS, "ldx sto")
        ph["S3"] = phase(GS, SUM, "ldg sto")
        ph["L3"] = phase(GS, "tr tg tc ev eg ec g0 sg0 th ot tn:2 w:3 y bn2 ag2 nw:13 apa so", "ldx ldg ldc sct:4")

        def finish(eng, name, but=()):
            q = ph[name]
            for k, n in q.end.items():
                if k in but or (isinstance(k, tuple) and k[0] in but):
                    continue
                eng.wait_ge(rg[k[0]][k[1]] if isinstance(k, tuple) else st[k], n)

        def begins_after(eng, *names):
            for n in names:
                finish(eng, n)

        X_, O_, A_ = 0, 32, 64
        A2_, A3_, A4_, A5_ = 80, 96, 112, 128
        G_ = 112
        MM_, MC_, DB_, OB_, QB_ = 0, 16, 32, 48, 72

        def osum(r):
            return flat(BUF[:, OB_:OB_ + 24, :])[:, r * 4 * (D + CNT):(r + 1) * 4 * (D + CNT)].rearrange(
                "p (t d) -> p t d", d=D + CNT)

        def cring(r):
            return flat(BUF[:, 16:18, :])[:, r * 4 * CNT:(r + 1) * 4 * CNT].rearrange("p (t k) -> p t k", k=CNT)

        oh = flat(BUF[:, 96:112, :])[:, 0:T * CNT].rearrange("p (t k) -> p t k", k=CNT)

        def raw(k, n=1):
            return BUF[:, k:k + n, :]
        RI = flat(BUF[:, 0:8, :]).bitcast(I32).rearrange("p (q h d) -> p q h d", h=2, d=D)
        RF = flat(BUF[:, 8:20, :]).rearrange("p (q h d) -> p q h d", h=2, d=D)
        R_W0, R_W1, R_WS, R_WN, R_WM, R_WIH, R_WHH, R_EMB, R_W1T, R_WIHT, R_EMBT, R_AA, R_GWS, R_GWN = (
            20, 21, 22, 23, 24, 25, 28, 31, 32, 33, 36, 37, 39, 40)

        def scr(k):
            return flat(BUF[:, 112 + 2 * k:114 + 2 * k, :])[:, 0:T]
        dP, penF, penB, va, vb, vc = scr(0), scr(1), scr(2), scr(3), scr(4), scr(5)
        sq_rows = [BUF[0:HT, 124:126, :], BUF[0:HT, 126:128, :]]

        def seq(t):
            return t.rearrange("(h p d) -> p h d", h=2, d=D)

        def seqp(t):
            return t.rearrange("(p t) -> p t", p=P)

        block = ctx.enter_context(nc.Block())

        @block.sync
        def _(sp):
            sp.wait_ge(*POOL.at("consts"))

            def ids(k, v, a0):
                n = E - a0
                full = n // D
                sp.dma_start(RI[0:HT, k, 0, :], v[a0:a0 + HT * D].rearrange("(p d) -> p d", d=D)).then_inc(loaded, 16)
                sp.dma_start(RI[0:full - HT, k, 1, :],
                             v[a0 + HT * D:a0 + full * D].rearrange("(p d) -> p d", d=D)).then_inc(loaded, 16)
                sp.dma_start(RI[full - HT:full - HT + 1, k, 1, 0:n - full * D],
                             v[a0 + full * D:E].rearrange("(p d) -> p d", p=1)).then_inc(loaded, 16)
            ids(0, dst, 0)
            ids(1, dst, 1)
            ids(2, src, 0)
            ids(3, etype, 0)
            with nc.allow_non_contiguous_dma(reason="biases as columns"):
                for k, v in ((G2, gamma2), (B2, beta2), (BM, b_msg), (A1, attn[0:D]), (A2, attn[D:2 * D])):
                    sp.dma_start(c(k), v.rearrange("(p o) -> p o", o=1)).then_inc(loaded, 16)
                sp.dma_start(c(BIH, 3), b_ih.rearrange("(c p) -> p c", p=D)).then_inc(loaded, 16)
                sp.dma_start(c(BHH, 3), b_hh.rearrange("(c p) -> p c", p=D)).then_inc(loaded, 16)
            for k, w in ((R_W0, w0), (R_W1, w1), (R_WS, w_self), (R_WN, w_neigh), (R_WM, w_msg)):
                sp.dma_start(raw(k)[:, 0, :], w).then_inc(loaded, 16)
            sp.dma_start(w1s[:, :], w1).then_inc(loaded, 16)
            sp.dma_start(raw(R_WIH, 3), w_ih.rearrange("(c p) f -> p c f", p=D)).then_inc(loaded, 16)
            sp.dma_start(raw(R_WHH, 3), w_hh.rearrange("(c p) f -> p c f", p=D)).then_inc(loaded, 16)
            sp.dma_start(raw(R_EMB)[0:TYPES, 0, :], embed).then_inc(loaded, 16)
            sp.dma_start(bias_r[:, 0, :], beta0.rearrange("(o f) -> o f", o=1)).then_inc(loaded, 16)
            sp.dma_start(row[:, 0, :], b2.rearrange("(o f) -> o f", o=1)).then_inc(loaded, 16)
            sp.dma_start(gam_b[:, :], gamma0.rearrange("(o f) -> o f", o=1).to_broadcast([P, D])).then_inc(loaded, 16)
            sp.wait_ge(*V.at("idf"))
            sp.dma_start(seq(dst_d), RF[0:HT, 0, :, :]).then_inc(bounce, 16)
            sp.wait_ge(bounce, 16)

            sp_pass = sem("sp_pass")

            def hold():
                sp.sem_inc(sp_pass, 1)

            def dense(name, load, store, lag):
                pipeline(sp, ph[name].steps, [(0, load), (lag, store)])

            def load_x(q, g, r, source, freed, first=X_):
                if q.old(g):
                    for k in freed:
                        sp.wait_ge(*q.done(k, g - R))
                        hold()
                ap = ring(first, r)
                if isinstance(g, int) and source.shape[0] < P:
                    ap = ap[0:source.shape[0]]
                sp.dma_start(ap, source).then_inc(rg["ldx"][r], 16)

            def store_nodes(q, g, r, table, first=O_, key="sto"):
                ap, dest = ring(first, r), table
                if dest.shape[0] < P:
                    ap = ap[0:dest.shape[0]]
                sp.dma_start(dest, ap).then_inc(rg[key][r], 16)

            sp.wait_ge(*V.at("wcx"))
            q = ph["A"]

            def load(g, r):
                load_x(q, g, r, nodes(x, g), ("xn", "y"))

            def store(g, r):
                sp.wait_ge(*q.done("apd", g))
                sp.wait_ge(*q.done("apa", g))
                hold()
                store_nodes(q, g, r, nodes(tab[1], g))
            dense("A", load, store, 6)

            def sums(name):
                q = ph[name]

                def load(g, r):
                    if q.old(g):
                        sp.wait_ge(*q.done("mk", g - R))
                        hold()
                    ids = dst_d[DS(g * 4 * D, 4 * D)] if not isinstance(g, int) else dst_d[g * 4 * D:(g + 1) * 4 * D]
                    sp.dma_start(flat(ring(DB_, r, 4)), ids.rearrange("(o f) -> o f", o=1).to_broadcast([P, 4 * D]))\
                        .then_inc(rg["ldg"][r], 16)

                def store(g, r):
                    if name in ("S1", "S2"):
                        sp.wait_ge(*q.done("qq", g))
                        hold()
                        sp.dma_start(tiles(slots(agg_d), g, 4), ring(QB_, r, 4)).then_inc(rg["sto"][r], 16)
                    else:
                        sp.wait_ge(*q.done("cv", g))
                        hold()
                        sp.dma_start(tiles(slots(agg_d), g, 4), osum(r)[:, :, 0:D]).then_inc(rg["sto"][r], 16)
                        if name == "S0":
                            sp.dma_start(tiles(slots(cnt_d), g, 4), osum(r)[:, :, D:]).then_inc(rg["sto"][r], 16)
                pipeline(sp, q.steps, [(0, load), (2, store)])
                finish(sp, name)

            def slot_phase(name, k, freed_x, freed_g, done, lag, w=W):
                q = ph[name]

                def load(g, r):
                    load_x(q, g, r, tiles(slots(xs[k]), g, W), freed_x)
                    if q.old(g):
                        for n in freed_g:
                            sp.wait_ge(*q.done(n, g - R))
                            hold()
                    sp.dma_start(ring(G_, r, W) if k else ring(G_, r, W), tiles(slots(agg_d), g, W))\
                        .then_inc(rg["ldg"][r], 16)

                def store(g, r):
                    for n in done:
                        sp.wait_ge(*q.done(n, g))
                        hold()
                    sp.dma_start(tiles(slots(xs[k + 1]), g, W), ring(O_, r)).then_inc(rg["sto"][r], 16)
                pipeline(sp, q.steps, [(0, load), (lag, store)])
                finish(sp, name)

            finish(sp, "A")
            sums("S0")
            finish(sp, "GD")
            slot_phase("L0", 0, ("y",), ("tr",), ("apd", "apa"), 7)

            q = ph["B"]

            def load(g, r):
                load_x(q, g, r, nodes(tab[1], g), ("bn1", "xn"))

            def store2(g, r):
                sp.wait_ge(*q.done("xn", g))
                hold()
                store_nodes(q, g, r, nodes(tab[2], g), A_, "st2")

            def store3(g, r):
                sp.wait_ge(*q.done("apd", g))
                sp.wait_ge(*q.done("apa", g))
                hold()
                store_nodes(q, g, r, nodes(tab[3], g))
            pipeline(sp, q.steps, [(0, load), (3, store2), (7, store3)])
            finish(sp, "B")

            n = 16

            def bring(dest, source, *wait):
                nonlocal n
                for w in wait:
                    sp.wait_ge(*w)
                sp.dma_start(dest, source).then_inc(bounce, 16)
                n += 16
                sp.wait_ge(bounce, n)
                sp.sem_inc(SPQ, 1)

            with nc.allow_non_contiguous_dma(reason="a column of 128 values"):
                def across(tag):
                    bring(row_d[:], vb[:, T - 1:T] if tag == "b" else vb[:, 0:1], SEQ.at(f"{tag}0"))
                    bring(row[:, 1, :], row_d[:].rearrange("(o f) -> o f", o=1))
                    bring(row2_d[:], row[:, 3, :], SEQ.at(f"{tag}2"))
                    bring(c(CC), row2_d[:].rearrange("(p o) -> p o", o=1))

                bring(dP, seqp(dst_d))
                bring(row_d[:], dP[:, 0:1])
                bring(row[:, 4, :], row_d[:].rearrange("(o f) -> o f", o=1))
                bring(row2_d[:], dP[:, T - 1:T])
                bring(row[:, 5, :], row2_d[:].rearrange("(o f) -> o f", o=1))
                bring(seq(seq_d), sq_rows[0], V.at("seqv"))
                bring(va, seqp(seq_d))
                across("a")
                bring(seqp(seq2_d), vc, SEQ.at("a5"))
                bring(sq_rows[1], seq(seq2_d))
                bring(seq(seq_d), sq_rows[0], V.at("seqe"))
                bring(va, seqp(seq_d))
                across("b")
                across("c")
                bring(seqp(seq2_d), vc, SEQ.at("c5"))
                bring(sq_rows[1], seq(seq2_d))

            sums("S1")
            slot_phase("L1", 1, ("y",), ("tr",), ("apd", "apa"), 4)

            def last_layer(name, g0):
                q = ph[name]

                def load(g, r):
                    load_x(q, g, r, nodes(tab[3], g + g0), ("y",))

                def store(g, r):
                    sp.wait_ge(*q.done("apa", g))
                    hold()
                    store_nodes(q, g, r, nodes(out, g + g0))
                dense(name, load, store, 7)
                finish(sp, name)

            last_layer("C1", 0)
            sums("S2")
            slot_phase("L2", 2, ("y", "u"), ("tg",), ("apd", "apa"), 6)
            last_layer("C2", C1N)
            sums("S3")

            q = ph["L3"]

            def load(g, r):
                if q.old(g):
                    sp.wait_ge(*q.done("y", g - R))
                    hold()
                sp.dma_start(ring(X_, r, 4), tiles(slots(xs[3]), g, 4)).then_inc(rg["ldx"][r], 16)
                if q.old(g):
                    sp.wait_ge(*q.done("tg", g - R))
                    hold()
                sp.dma_start(ring(G_, r, 4), tiles(slots(agg_d), g, 4)).then_inc(rg["ldg"][r], 16)
                if q.old(g):
                    sp.wait_ge(*q.done("tc", g - R))
                    hold()
                sp.dma_start(cring(r), tiles(slots(cnt_d), g, 4)).then_inc(rg["ldc"][r], 16)
            pipeline(sp, q.steps, [(0, load)])
            finish(sp, "L3")

        @block.gpsimd
        def _(pool):
            g_ = nc.gpsimd

            def hold():
                pool.sem_inc(pool_pass, 1)

            g_.memset(flat(BUF[:, 0:2, :]).bitcast(I32), -5)
            g_.memset(flat(BUF[:, 2:4, :]).bitcast(I32), -5)
            g_.memset(flat(BUF[:, 4:8, :]).bitcast(I32), 0)
            g_.memset(epsc[:, :], EPS)
            g_.memset(onesf[:, :], 1.0)
            g_.memset(ident[:, :], 0.0)
            POOL.did(g_.memset(e127[:, :], 0.0), "consts")
            pool.wait_ge(*POOL.at("consts"))
            g_.affine_select(out=e127[:, :], in_=e127[:, :], compare_op=ALU.not_equal, fill=1.0, base=-(P - 1),
                             pattern=[[0, 1]], channel_multiplier=1)
            POOL.did(g_.affine_select(out=ident[:, :], in_=ident[:, :], compare_op=ALU.not_equal, fill=1.0, base=0,
                                      pattern=[[-1, P]], channel_multiplier=1), "ident")

            def gather(name, index, table, dest):
                q = ph[name]

                def fetch(g, r):
                    if q.old(g):
                        pool.wait_ge(*q.moved("plc", g - R, r))
                        hold()
                    g_.tensor_copy(iring[:, r, :], tiles(index, g, 4)).then_inc(st["ix"], 1)
                    pool.wait_ge(*q.done("ix", g))
                    hold()
                    for j in range(4):
                        g_.indirect_dma_start(out=gring[:, r, j, :], out_offset=None, in_=table[:, :],
                                              in_offset=bass.IndirectOffsetOnAxis(ap=iring[:, r, j:j + 1], axis=0))\
                            .then_inc(rg["gat"][r], 16)

                def place(g, r):
                    pool.wait_ge(*q.moved("gat", g, r))
                    hold()
                    g_.dma_start(tiles(dest, g, 4), gring[:, r, :, :]).then_inc(rg["plc"][r], 16)
                pipeline(pool, q.steps, [(0, fetch), (2, place)])
                finish(pool, name, ("ix",))
                hold()

            def scatter(name, table, n, done, lag):
                q = ph[name]

                def put(g, r):
                    if q.old(g):
                        pool.wait_ge(*q.moved("sct", g - R, r))
                        hold()
                    g_.tensor_copy(oring[:, r, 0:n], tiles(sci, g, n)).then_inc(st["so"], 1)
                    pool.wait_ge(*q.done("so", g))
                    hold()
                    for k in done:
                        pool.wait_ge(*q.done(k, g))
                        hold()
                    for j in range(n):
                        g_.indirect_dma_start(out=table[:, :],
                                              out_offset=bass.IndirectOffsetOnAxis(ap=oring[:, r, j:j + 1], axis=0),
                                              in_=ring(O_, r, n)[:, j, :], in_offset=None,
                                              bounds_check=N - 1, oob_is_err=False).then_inc(rg["sct"][r], 16)
                pipeline(pool, q.steps, [(0, put)])
                finish(pool, name)
                hold()

            pool.wait_ge(*V.at("idx"))
            gather("G0", srci, x, S)
            gather("GD", dgi, x, slots(xs[0]))
            finish(pool, "A")
            scatter("L0", tab[1], 8, ("apd", "apa"), 4)
            gather("G1", srci, tab[1], S)
            finish(pool, "B")
            scatter("L1", tab[2], 8, ("apd", "apa"), 3)
            gather("G2", srci, tab[2], S)
            finish(pool, "C1")
            scatter("L2", tab[3], 8, ("apd", "apa"), 4)
            gather("G3", srci, tab[3], S)
            finish(pool, "C2")
            scatter("L3", out, 4, ("apa",), 0)

        def gated_rings(slot):
            if slot:
                return (lambda r: ring(48, r, 4), lambda r: ring(72, r % 2, 4), lambda r: ring(80, r % 2, 4),
                        lambda r: ring(96, r % 2, 4))
            return (lambda r: ring(64, r), lambda r: ring(112, r % 2), lambda r: ring(128, r % 2),
                    lambda r: ring(96, r % 2))

        BFWD = 4

        @block.vector
        def _(dve):
            v = nc.vector
            own = sem("dve_own")
            dpass = sem("dve_pass")
            cnt = 0

            def hold():
                dve.sem_inc(dpass, 1)

            def do(ins):
                nonlocal cnt
                ins.then_inc(own, 1)
                cnt += 1
                dve.wait_ge(own, cnt)

            def step(ins, name, steps=V):
                steps.did(ins, name)
                dve.wait_ge(*steps.at(name))

            dve.wait_ge(loaded, 16 * 31)
            do(v.tensor_copy(RF[0:HT, 0:4], RI[0:HT, 0:4]))
            do(v.tensor_tensor(RF[0:HT, 4], RF[0:HT, 0], RF[0:HT, 1], ALU.not_equal))
            do(v.scalar_tensor_tensor(RF[0:HT, 5], RF[0:HT, 0], float(-BIG), RF[0:HT, 4], ALU.add, ALU.mult))
            step(v.tensor_scalar(RF[0:HT, 5], RF[0:HT, 5], float(BIG), None, ALU.add), "idf")
            dve.wait_ge(*PEQ.at("ids"))
            do(v.tensor_copy(dstc[:, :], PS[:, 0, 0:T]))
            do(v.tensor_copy(srci[:, :], PS[:, 2, 0:T]))
            do(v.tensor_scalar(typec[:, :], PS[:, 3, 0:T], 0.0, float(TYPES - 1), ALU.max, ALU.min))
            do(v.tensor_copy(lastc[:, :], PS[:, 4, 0:T]))
            do(v.tensor_copy(sci[:, :], PS[:, 5, 0:T]))
            step(v.tensor_scalar(dgi[:, :], dstc[:, :], 0.0, None, ALU.max), "idx")
            dve.wait_ge(*POOL.at("ident"))
            do(v.memset(dprev[:, :], -1.0))
            do(v.tensor_scalar(dprev[:, 1:T], dstc[:, 0:T - 1], 1.0, e127[:, 0:1], ALU.add, ALU.mult))
            do(v.tensor_scalar(dprev[:, 1:T], dprev[:, 1:T], -1.0, None, ALU.add))
            do(v.tensor_scalar(cen[:, :], ident[:, :], -1.0 / D, None, ALU.add))
            do(v.tensor_scalar(raw(R_AA)[:, 0, :], onesf[:, :], c(A1), None, ALU.mult))
            do(v.tensor_scalar(raw(R_AA + 1)[:, 0, :], onesf[:, :], c(A2), None, ALU.mult))
            do(v.tensor_scalar(raw(R_GWS)[:, 0, :], raw(R_WS)[:, 0, :], c(G2), None, ALU.mult))
            do(v.tensor_scalar(raw(R_GWN)[:, 0, :], raw(R_WN)[:, 0, :], c(G2), None, ALU.mult))
            do(v.tensor_tensor(c(BR), c(BIH), c(BHH), ALU.add))
            step(v.tensor_tensor(c(BZ), c(BIH + 1), c(BHH + 1), ALU.add), "cen")
            dve.wait_ge(*PEQ.at("emb"))
            do(v.tensor_copy(w0T[:, :], PS[:, 0, 0:D]))
            do(v.tensor_copy(whT[:, :], PS[:, 1, 0:3 * D]))
            do(v.tensor_copy(flat(raw(R_WIHT, 3)), PS[:, 2, 0:3 * D]))
            do(v.tensor_copy(raw(R_W1T)[:, 0, :], PS[:, 3, 0:D]))
            step(v.tensor_scalar(raw(R_EMBT)[:, 0, 0:TYPES], PS[:, 4, 0:TYPES], c(BM), None, ALU.add), "embc")
            dve.wait_ge(*PEQ.at("wcx"))
            do(v.tensor_copy(wsc[:, :], PS[:, 5, 0:D]))
            do(v.tensor_copy(wnc[:, :], PS[:, 5, D:2 * D]))
            do(v.tensor_copy(flat(wa_b), PS[:, 6, 0:2 * D]))
            do(v.tensor_tensor(bias_r[:, 1, :], PS[0:1, 7, 0:D], row[:, 0, :], ALU.add))
            do(v.tensor_tensor(bias_r[:, 2, :], PS[0:1, 7, D:2 * D], bias_r[:, 1, :], ALU.add))
            do(v.tensor_copy(wcT[:, :], PS[:, 0, 0:3 * D]))
            do(v.tensor_copy(wcE[:, :], PS[0:TYPES, 1, 0:3 * D]))
            dve.wait_ge(bounce, 16)
            step(v.memset(flat(BUF[:, :, :]), 0.0), "wcx")

            def bn_stage(q, name, stats, source, *needs):
                def f(g, r):
                    for n in needs:
                        dve.wait_ge(*n(g, r))
                    src_ = source(r)
                    n_ = src_.shape[1]
                    for j in range(n_):
                        ins = v.bn_stats(stats[:, j, :], src_[:, j, :])
                    ins.then_inc(st[name], 1)
                return f

            def ag_stage(q, name, after, stats, mv, n=W):
                def f(g, r):
                    dve.wait_ge(*q.done(after, g))
                    hold()
                    for j in range(n):
                        ins = v.bn_aggr(mv[:, r, j, :], stats[:, j, :])
                    ins.then_inc(st[name], 1)
                return f

            def rc_stage(q, name, after, root, inv):
                def f(g, r):
                    dve.wait_ge(*q.done(after, g))
                    v.reciprocal(inv[:, r, :], root[:, r, :]).then_inc(st[name], 1)
                return f

            def nm_stage(q, name, after, mv, inv, nm):
                def f(g, r):
                    dve.wait_ge(*q.done(after, g))
                    v.scalar_tensor_tensor(nm[:, r, :], mv[:, r, :, 0], -1.0, inv[:, r, :], ALU.mult, ALU.mult)\
                        .then_inc(st[name], 1)
                return f

            def apply_stage(q, source, scatters=False, extra=()):
                def f(g, r):
                    dve.wait_ge(*q.done("nm2", g))
                    if q.old(g):
                        dve.wait_ge(*q.moved("sto", g - R, r))
                        if scatters:
                            dve.wait_ge(*q.moved("sct", g - R, r))
                        for n in extra:
                            dve.wait_ge(*q.done(n, g - R))
                    for j in range(BFWD):
                        ins = v.tensor_scalar(ring(O_, r)[:, j, :], source(r)[:, j, :], rs2[:, r, j:j + 1],
                                              nm2[:, r, j:j + 1], ALU.mult, ALU.add)
                    ins.then_inc(st["apd"], 1)
                return f

            def ybank(b0):
                return lambda r: wide(b0 + 2 * (r % 2))

            def bc(t, r, n=W):
                return t[:, r, 0:n].unsqueeze(2).to_broadcast([P, n, D])

            def first_layer(name):
                q = ph[name]
                slot = name == "L0"
                o = 1 if slot else 0
                H = lambda r: ring(A3_, r % 2)
                XN = lambda r: ring(A_, r % 2)

                def relu(g, r):
                    dve.wait_ge(*q.done("h", g))
                    dve.wait_ge(*q.moved("ldx", g, r))
                    if q.old(g, 2):
                        dve.wait_ge(*q.done("xn", g - 2))
                    v.scalar_tensor_tensor(H(r), wide(6), 0.0, ring(X_, r), ALU.max, ALU.add).then_inc(st["rel"], 1)

                def gamma(g, r):
                    dve.wait_ge(*q.done("xn", g))
                    v.tensor_tensor(XN(r), XN(r), gam_b[:, :].unsqueeze(1).to_broadcast([P, W, D]), ALU.mult)\
                        .then_inc(st["gm"], 1)

                prod = gring[:, 0:2, :, :].rearrange("p a b d -> p (a b) d")

                def sdots(g, r):
                    if q.old(g, 1):
                        dve.wait_ge(*q.done("sdp", g - 1))
                    dve.wait_ge(*q.done("apd", g))
                    dve.wait_ge(*q.done("apa", g))
                    v.tensor_tensor(prod, ring(O_, r), wa_b[:, 1, :].unsqueeze(1).to_broadcast([P, W, D]),
                                    ALU.mult).then_inc(st["sdp"], 1)
                    dve.wait_ge(*q.done("sdp", g, 1))
                    hold()
                    v.tensor_reduce(tiles(sD, g, W), prod, AX, ALU.add).then_inc(st["sdp"], 1)

                bn1 = bn_stage(q, "bn1", st1, H if slot else (lambda r: ring(X_, r)),
                               (lambda g, r: q.done("rel", g)) if slot else (lambda g, r: q.moved("ldx", g, r)))
                bn2 = bn_stage(q, "bn2", st2, ybank(0), lambda g, r: q.done("y", g))
                stages = [
                    (1 + o, rc_stage(q, "rc1", "sq1", sd1, rs1)),
                    (4 + o, rc_stage(q, "rc2", "sq2", sd2, rs2)),
                    (2 + o, gamma),
                    (4 + o, nm_stage(q, "nm2", "rc2", mv2, rs2, nm2)),
                    (1 + o, nm_stage(q, "nm1", "rc1", mv1, rs1, nm1)),
                    (4 + o, apply_stage(q, ybank(0), slot, ("sdp",) if slot else ()))] + ([(1, relu)] if slot else []) + [
                    (o, bn1), (3 + o, bn2),
                    (o, ag_stage(q, "ag1", "bn1", st1, mv1)),
                    (3 + o, ag_stage(q, "ag2", "bn2", st2, mv2))] + ([(5 + o, sdots)] if slot else [])
                pipeline(dve, q.steps, stages)
                finish(dve, name)

            def sums(name, weight=None):
                q = ph[name]

                def match(g, r):
                    dve.wait_ge(*q.moved("ldg", g, r))
                    if q.old(g):
                        dve.wait_ge(*q.done("sm", g - R))
                    for j in range(4):
                        one = lambda t: t[:, DS(g * 4 + j, 1)] if not isinstance(g, int) else t[:, g * 4 + j:g * 4 + j + 1]
                        ids = ring(DB_, r, 4)[:, j, :]
                        if weight is None:
                            v.tensor_scalar(ring(MM_, r, 4)[:, j, :], ids, one(dstc), None, ALU.is_equal)
                        else:
                            v.tensor_scalar(ring(MM_, r, 4)[:, j, :], ids, one(dstc), one(weight), ALU.is_equal, ALU.mult)
                        ins = v.tensor_scalar(ring(MC_, r, 4)[:, j, :], ids, one(dprev), None, ALU.is_equal)
                    ins.then_inc(st["mk"], 1)

                def scale(g, r):
                    dve.wait_ge(*q.done("cv", g))
                    if name == "S0":
                        hold()
                        v.reciprocal(tiles(rdeg, g, 4), osum(r)[:, :, D + TYPES]).then_inc(st["qq"], 1)
                        return
                    if name == "S1":
                        v.tensor_scalar(nm1[:, r, 0:4], osum(r)[:, :, D], 1e-6, None, ALU.max).then_inc(st["qq"], 1)
                        dve.wait_ge(*q.done("qq", g, 1))
                        v.reciprocal(rs1[:, r, 0:4], nm1[:, r, 0:4]).then_inc(st["qq"], 1)
                        dve.wait_ge(*q.done("qq", g, 2))
                        by = bc(rs1, r, 4)
                    else:
                        by = tiles(rdeg, g, 4).unsqueeze(2).to_broadcast([P, 4, D])
                    if q.old(g):
                        dve.wait_ge(*q.moved("sto", g - R, r))
                    v.tensor_tensor(ring(QB_, r, 4), osum(r)[:, :, 0:D], by, ALU.mult).then_inc(st["qq"], 1)
                pipeline(dve, q.steps, [(0, match)] + ([(1, scale)] if name != "S3" else []))
                finish(dve, name)

            first_layer("A")
            finish(dve, "G0")
            for k in range(TYPES):
                do(v.tensor_scalar(oh[:, :, k], typec[:, :], float(k), None, ALU.is_equal))
            step(v.memset(oh[:, :, TYPES], 1.0), "oh")
            sums("S0")
            finish(dve, "GD")
            first_layer("L0")

            q = ph["B"]

            def q0(g, r):
                dve.wait_ge(*q.done("rc1", g))
                v.tensor_tensor(rs3[:, r, :], rs1[:, r, :], rs1[:, r, :], ALU.mult).then_inc(st["q"], 1)

            def q1(g, r):
                dve.wait_ge(*q.done("q", g, 1))
                v.tensor_tensor(rs3[:, r, :], rs3[:, r, :], mv1[:, r, :, 1], ALU.mult).then_inc(st["q"], 1)

            def u(g, r):
                dve.wait_ge(*q.done("r3", g))
                dve.wait_ge(*q.done("xn", g))
                if q.old(g, 2):
                    dve.wait_ge(*q.done("tr", g - 2))
                v.tensor_tensor(ring(A3_, r % 2), ring(A_, r), bc(rs3, r), ALU.mult).then_inc(st["u"], 1)
            pipeline(dve, q.steps, [
                (1, rc_stage(q, "rc1", "sq1", sd1, rs1)),
                (2, rc_stage(q, "r3", "sq3", sd3, rs3)),
                (5, rc_stage(q, "rc2", "sq2", sd2, rs2)),
                (0, bn_stage(q, "bn1", st1, lambda r: ring(X_, r), lambda g, r: q.moved("ldx", g, r))),
                (1, q0),
                (1, nm_stage(q, "nm1", "rc1", mv1, rs1, nm1)),
                (5, nm_stage(q, "nm2", "rc2", mv2, rs2, nm2)),
                (0, ag_stage(q, "ag1", "bn1", st1, mv1)),
                (1, q1),
                (2, u),
                (5, apply_stage(q, ybank(2))),
                (4, bn_stage(q, "bn2", st2, ybank(2), lambda g, r: q.done("y", g))),
                (4, ag_stage(q, "ag2", "bn2", st2, mv2))])
            finish(dve, "B")

            finish(dve, "G1")
            ssq = sem("ssq")

            def dots(g, r):
                v.tensor_tensor(ring(X_, 0), tiles(S, g, W), wa_b[:, 0, :].unsqueeze(1).to_broadcast([P, W, D]),
                                ALU.mult).then_inc(ssq, 1)
                dve.wait_ge(ssq, g * 2 + 1)
                hold()
                v.tensor_reduce(tiles(sS, g, W), ring(X_, 0), AX, ALU.add).then_inc(ssq, 1)
                dve.wait_ge(ssq, g * 2 + 2)
                hold()
            pipeline(dve, T // W, [(0, dots)])
            do(v.tensor_tensor(sD[:, :], sD[:, :], lastc[:, :], ALU.mult))
            do(v.tensor_scalar(mx[:, :], lastc[:, :], -1.0, NEG, ALU.add, ALU.mult))
            step(v.tensor_tensor(sD[:, :], sD[:, :], mx[:, :], ALU.add), "sDv")
            dve.wait_ge(SPQ, 5)
            do(v.tensor_tensor(penF[:, 1:T], dP[:, 1:T], dP[:, 0:T - 1], ALU.is_equal))
            do(v.tensor_scalar(penF[:, 1:T], penF[:, 1:T], -1.0, NEG, ALU.add, ALU.mult))
            do(v.memset(penF[:, 0:1], -NEG))
            do(v.tensor_copy(penB[:, 0:T - 1], penF[:, 1:T]))
            do(v.memset(penB[:, T - 1:T], -NEG))
            rw = lambda k: row[:, k, :]
            do(v.memset(rw(6), -NEG))
            do(v.tensor_tensor(row[:, 6, 1:P], row[:, 4, 1:P], row[:, 5, 0:P - 1], ALU.is_equal))
            do(v.tensor_scalar(row[:, 6, 1:P], row[:, 6, 1:P], -1.0, NEG, ALU.add, ALU.mult))
            do(v.tensor_tensor(rw(7), rw(4), rw(5), ALU.is_equal))
            do(v.tensor_scalar(rw(7), rw(7), -1.0, NEG, ALU.add, ALU.mult))
            do(v.tensor_tensor(rw(4), rw(7), rw(6), ALU.add))
            do(v.memset(rw(5), -NEG))
            do(v.tensor_tensor(row[:, 5, 0:P - 1], row[:, 7, 0:P - 1], row[:, 6, 1:P], ALU.add))
            do(v.memset(rw(3), -NEG))

            def scan(dst_, pen, val, back):
                if back:
                    return v.tensor_tensor_scan(dst_[:, ::-1], pen[:, ::-1], val[:, ::-1], -NEG, ALU.add, ALU.max)
                return v.tensor_tensor_scan(dst_, pen, val, -NEG, ALU.add, ALU.max)

            def spread(tag, back, first):
                pen = penB if back else penF
                step(scan(vb, pen, va, back), tag + "0", SEQ)
                dve.wait_ge(SPQ, first + 2)
                do(scan(rw(2), rw(5) if back else rw(4), rw(1), back))
                if back:
                    do(v.memset(row[:, 3, P - 1:P], -NEG))
                    step(v.tensor_tensor(row[:, 3, 0:P - 1], row[:, 2, 1:P], row[:, 6, 1:P], ALU.add), tag + "2", SEQ)
                else:
                    do(v.memset(row[:, 3, 0:1], -NEG))
                    step(v.tensor_tensor(row[:, 3, 1:P], row[:, 2, 0:P - 1], row[:, 6, 1:P], ALU.add), tag + "2", SEQ)
                dve.wait_ge(SPQ, first + 4)
                at = slice(T - 1, T) if back else slice(0, 1)
                do(v.tensor_tensor(va[:, at], va[:, at], c(CC), ALU.max))
                return scan(vc, pen, va, back)

            dve.wait_ge(*PEQ.at("sdv"))
            step(v.tensor_copy(flat(sq_rows[0]), PS[0:HT, 0, 0:2 * D]), "seqv")
            dve.wait_ge(SPQ, 7)
            step(spread("a", True, 7), "a5", SEQ)
            dve.wait_ge(*PEQ.at("sdb"))
            do(v.tensor_tensor(sS[:, :], sS[:, :], PS[:, 1, 0:T], ALU.add))
            step(v.scalar_tensor_tensor(sS[:, :], sS[:, :], SLOPE, sS[:, :], ALU.mult, ALU.max), "e")
            dve.wait_ge(*PEQ.at("ev"))
            step(v.tensor_copy(flat(sq_rows[0]), PS[0:HT, 2, 0:2 * D]), "seqe")
            dve.wait_ge(SPQ, 15)
            do(spread("b", False, 15))
            do(v.tensor_copy(va, vc))
            step(spread("c", True, 19), "c5", SEQ)
            dve.wait_ge(*PEQ.at("mb"))
            step(v.tensor_tensor(ew[:, :], sS[:, :], PS[:, 3, 0:T], ALU.subtract), "exa")
            dve.wait_ge(*ACQ.at("exp"))
            sums("S1", ew)

            q = ph["L1"]
            pipeline(dve, q.steps, [
                (2, rc_stage(q, "rc2", "sq2", sd2, rs2)),
                (1, bn_stage(q, "bn2", st2, ybank(2), lambda g, r: q.done("y", g))),
                (2, nm_stage(q, "nm2", "rc2", mv2, rs2, nm2)),
                (1, ag_stage(q, "ag2", "bn2", st2, mv2)),
                (2, apply_stage(q, ybank(2), True))])
            finish(dve, "L1")

            def newton(q, k, g, r, n):
                if k:
                    dve.wait_ge(*q.done("nw", g, k))
                else:
                    dve.wait_ge(*q.done("ag2", g))
                vv, tt, yy = nwt[:, 0, 0:n], nwt[:, 1, 0:n], rs2[:, r, 0:n]
                if k == 0:
                    ins = v.tensor_scalar(vv, mv2[:, r, 0:n, 1], EPS, None, ALU.add)
                elif k == 1:
                    ins = v.tensor_scalar(nwi[:, 0:n], vv.bitcast(I32), 1, None, ALU.logical_shift_right)
                elif k == 2:
                    ins = v.tensor_scalar(yy.bitcast(I32), nwi[:, 0:n], -1.0, MAGIC, ALU.mult, ALU.add)
                elif k == 12:
                    ins = v.scalar_tensor_tensor(nm2[:, r, 0:n], mv2[:, r, 0:n, 0], -1.0, yy, ALU.mult, ALU.mult)
                elif k % 3 == 0:
                    ins = v.tensor_tensor(tt, yy, yy, ALU.mult)
                elif k % 3 == 1:
                    ins = v.scalar_tensor_tensor(tt, tt, -0.5, vv, ALU.mult, ALU.mult)
                else:
                    ins = v.scalar_tensor_tensor(yy, tt, 1.5, yy, ALU.add, ALU.mult)
                ins.then_inc(st["nw"], 1)

            def gated(name):
                q = ph[name]
                slot = name == "L3"
                n = 4 if slot else W
                halves = 1 if slot else 2
                XT, RN, Z, Y = gated_rings(slot)

                def y(g, r):
                    dve.wait_ge(*q.done("ot", g))
                    if q.old(g, 2):
                        dve.wait_ge(*q.done("apa", g - 2))
                    source = PS[:, 3, :].rearrange("p (t d) -> p t d", d=D) if slot else wide(0)
                    v.tensor_tensor(Y(r), source, ring(X_, r, n), ALU.add).then_inc(st["y"], 1)

                def w(k):
                    def f(g, r):
                        dve.wait_ge(*(q.done("w", g, k) if k else q.done("th", g)))
                        if k == 0:
                            ins = v.tensor_tensor(XT(r), XT(r), RN(r), ALU.subtract)
                        elif k == 1:
                            ins = v.tensor_tensor(XT(r), XT(r), Z(r), ALU.mult)
                        else:
                            ins = v.tensor_tensor(XT(r), XT(r), RN(r), ALU.add)
                        ins.then_inc(st["w"], 1)
                    return f

                def tn(h):
                    def f(g, r):
                        dve.wait_ge(*q.done(f"sg{h}", g))
                        a = flat(RN(r))[:, 512 * h:512 * (h + 1)]
                        v.scalar_tensor_tensor(a, PS[:, 6 if slot else 4 + 3 * h, :], c(BHH + 2), a, ALU.add, ALU.mult)\
                            .then_inc(st["tn"], 1)
                    return f

                def tn_in(g, r):
                    dve.wait_ge(*q.done("tn", g, 1))
                    v.tensor_tensor(flat(RN(r)), flat(RN(r)), PS[:, 7, :], ALU.add).then_inc(st["tn"], 1)

                def nw(*ks):
                    def f(g, r):
                        for k in ks:
                            if q.old(g) and k == 2:
                                dve.wait_ge(*q.done("apa", g - R))
                            newton(q, k, g, r, n)
                    return f
                bn = bn_stage(q, "bn2", st2, Y, lambda g, r: q.done("y", g))
                pipeline(dve, q.steps, [
                    (3, y), (4, nw(0)), (2, w(0)), (4, nw(1)), (2, w(1)), (4, nw(2)), (2, w(2)), (4, nw(3)),
                    (1, tn(0)), (4, nw(4)), (1, tn_in if slot else tn(1)), (4, nw(5)),
                    (3, bn), (4, nw(6, 7, 8, 9, 10, 11, 12)), (3, ag_stage(q, "ag2", "bn2", st2, mv2, n))])
                finish(dve, name)

            gated("C1")

            finish(dve, "G2")
            vsq = sem("vsq")

            def row_var(g, r):
                if q.old(g, 1):
                    dve.wait_ge(vsq, g * 3)
                    hold()
                for j in range(W):
                    one = S[:, DS(g * W + j, 1), :] if not isinstance(g, int) else S[:, g * W + j:g * W + j + 1, :]
                    ins = v.bn_stats(st1[:, j, :], one.rearrange("p o d -> p (o d)"))
                ins.then_inc(vsq, 1)
                dve.wait_ge(vsq, g * 3 + 1)
                hold()
                for j in range(W):
                    ins = v.bn_aggr(mv1[:, 0, j, :], st1[:, j, :])
                ins.then_inc(vsq, 1)
                dve.wait_ge(vsq, g * 3 + 2)
                hold()
                v.tensor_scalar(tiles(mx, g, W), mv1[:, 0, :, 1], EPS, None, ALU.add).then_inc(vsq, 1)
            pipeline(dve, T // W, [(0, row_var)])
            dve.wait_ge(vsq, 3 * (T // W))
            hold()
            do(v.reciprocal(mx[:, :], mx[:, :]))
            step(v.tensor_copy(sD[:, :], mx[:, :]), "rv")
            dve.wait_ge(*ACQ.at("rv"))
            sums("S2", ew)

            q = ph["L2"]
            pipeline(dve, q.steps, [
                (1, rc_stage(q, "rc1", "sq1", sd1, rs1)),
                (4, rc_stage(q, "rc2", "sq2", sd2, rs2)),
                (0, bn_stage(q, "bn1", st1, lambda r: ring(X_, r), lambda g, r: q.moved("ldx", g, r))),
                (1, nm_stage(q, "nm1", "rc1", mv1, rs1, nm1)),
                (4, nm_stage(q, "nm2", "rc2", mv2, rs2, nm2)),
                (0, ag_stage(q, "ag1", "bn1", st1, mv1)),
                (4, apply_stage(q, ybank(2), True)),
                (3, bn_stage(q, "bn2", st2, ybank(2), lambda g, r: q.done("y", g))),
                (3, ag_stage(q, "ag2", "bn2", st2, mv2))])
            finish(dve, "L2")
            gated("C2")
            finish(dve, "G3")
            sums("S3")
            gated("L3")

        @block.tensor
        def _(pe):
            te = nc.tensor
            pe.wait_ge(*POOL.at("ident"))
            pe.wait_ge(*V.at("idf"))
            for k in (0, 2, 3, 4, 5):
                for h in range(2):
                    ins = te.transpose(PS[:, k, h * HT:(h + 1) * HT], RF[0:HT, k, h, :], ident[0:HT, 0:HT])
            PEQ.did(ins, "ids")
            pe.wait_ge(*V.at("idx"))
            pe.wait_ge(*V.at("cen"))
            te.transpose(PS[:, 0, 0:D], raw(R_W0)[:, 0, :], ident[:, :])
            for k in range(3):
                te.transpose(PS[:, 1, k * D:(k + 1) * D], raw(R_WHH + k)[:, 0, :], ident[:, :])
                te.transpose(PS[:, 2, k * D:(k + 1) * D], raw(R_WIH + k)[:, 0, :], ident[:, :])
            te.transpose(PS[:, 3, 0:D], raw(R_W1)[:, 0, :], ident[:, :])
            PEQ.did(te.transpose(PS[:, 4, 0:TYPES], raw(R_EMB)[0:TYPES, 0, :], ident[0:TYPES, 0:TYPES]), "emb")

            def mm(o, a, b, start=True, stop=True):
                return te.matmul(o, a, b, start=start, stop=stop)
            mm(PS[:, 5, 0:D], cen[:, :], raw(R_GWS)[:, 0, :])
            mm(PS[:, 5, D:2 * D], cen[:, :], raw(R_GWN)[:, 0, :])
            pe.wait_ge(*V.at("embc"))
            for k in range(2):
                mm(PS[:, 6, k * D:(k + 1) * D], raw(R_AA + k)[:, 0, :], raw(R_W1T)[:, 0, :])
            mm(PS[0:1, 7, 0:D], c(B2), raw(R_WS)[:, 0, :])
            mm(PS[0:1, 7, D:2 * D], c(B2), raw(R_WN)[:, 0, :])
            mm(PS[:, 0, 0:3 * D], raw(R_WM)[:, 0, :], flat(raw(R_WIHT, 3)))
            PEQ.did(mm(PS[0:TYPES, 1, 0:3 * D], raw(R_EMBT)[:, 0, 0:TYPES], flat(raw(R_WIHT, 3))), "wcx")
            pe.wait_ge(*V.at("wcx"))

            def turn(o, source, n):
                for j in range(n):
                    ins = te.transpose(o[:, j, :], source[:, j, :], ident[:, :])
                return ins

            def total(q, b, x_, terms, bias):
                for h in range(2):
                    yo = wide(b)[:, 4 * h:4 * h + 4, :]
                    mm(yo, ident[:, :], x_[:, 4 * h:4 * h + 4, :], True, False)
                    if bias is not None:
                        mm(yo, onesf[0:1, :], bias_r[:, bias:bias + 1, :].to_broadcast([1, 4, D]), False, False)
                    for j in range(4 * h, 4 * h + 4):
                        for k, (left, right) in enumerate(terms):
                            ins = mm(wide(b)[:, j, :], left[:, j, :], right[:, :], False,
                                     k == len(terms) - 1 and j == 4 * h + 3)
                return ins

            def first_layer(name):
                q = ph[name]
                slot = name == "L0"
                o = 1 if slot else 0
                XN = lambda r: ring(A_, r % 2)
                base_rows = lambda r: ring(X_, r)

                def tr(g, r):
                    pe.wait_ge(*q.moved("ldg", g, r))
                    if q.old(g, 1):
                        pe.wait_ge(*q.done("ev", g - 1))
                    turn(wide(4), ring(G_, r), W).then_inc(st["tr"], 1)

                def h(g, r):
                    pe.wait_ge(*q.done("ev", g))
                    if q.old(g, 1):
                        pe.wait_ge(*q.done("rel", g - 1))
                    for j in range(W):
                        ins = mm(wide(6)[:, j, :], ring(A2_, r % 2)[:, j, :], w0T[:, :])
                    ins.then_inc(st["h"], 1)

                def y(g, r):
                    pe.wait_ge(*q.done("gm", g))
                    if q.old(g, 2):
                        pe.wait_ge(*q.done("apd", g - 2))
                        pe.wait_ge(*q.done("apa", g - 2))
                    b = 2 * (r % 2)
                    for hh in range(2):
                        yo = wide(b)[:, 4 * hh:4 * hh + 4, :]
                        mm(yo, ident[:, :], base_rows(r)[:, 4 * hh:4 * hh + 4, :], True, False)
                        mm(yo, onesf[0:1, :], bias_r[:, 0:1, :].to_broadcast([1, 4, D]), False, False)
                        ins = mm(yo, ident[:, :], XN(r)[:, 4 * hh:4 * hh + 4, :], False, True)
                    ins.then_inc(st["y"], 1)
                pipeline(pe, q.steps, ([(0, tr), (1, h)] if slot else []) + [(2 + o, y)])
                finish(pe, name)

            def sums(name, more=None, width=D):
                q = ph[name]

                def one(g, r):
                    pe.wait_ge(*q.done("mk", g))
                    for j in range(4):
                        k = g * 4 + j
                        t_ = (lambda a: a[:, DS(k, 1)]) if not isinstance(g, int) else (lambda a: a[:, k:k + 1])
                        m = ring(MM_, r, 4)[:, j, :]
                        rows_ = t_(S).rearrange("p o d -> p (o d)")
                        mm(PS[:, j % 2, 0:D], m, rows_, True, False)
                        if more is not None:
                            mm(PS[:, j % 2, D:width], m, more(t_), False, False)
                        if j or not isinstance(g, int) or g:
                            pe.wait_ge(*q.done("cv", g, j))
                        last_ = osum(r)[:, j - 1, 0:width] if j else osum((r - 1) % R)[:, 3, 0:width]
                        mm(PS[:, j % 2, 0:width], ring(MC_, r, 4)[:, j, :], last_, False, True).then_inc(st["sm"], 1)
                pipeline(pe, q.steps, [(0, one)])
                finish(pe, name)

            first_layer("A")
            finish(pe, "G0")
            pe.wait_ge(*V.at("oh"))
            sums("S0", lambda t_: t_(oh).rearrange("p o d -> p (o d)"), D + CNT)
            first_layer("L0")

            q = ph["B"]

            def trB(g, r):
                pe.wait_ge(*q.done("u", g))
                if q.old(g, 1):
                    pe.wait_ge(*q.done("ev", g - 1))
                turn(wide(0), ring(A3_, r % 2), W).then_inc(st["tr"], 1)

            def yB(g, r):
                pe.wait_ge(*q.done("ev", g))
                if q.old(g, 2):
                    pe.wait_ge(*q.done("apd", g - 2))
                    pe.wait_ge(*q.done("apa", g - 2))
                total(q, 2 + 2 * (r % 2), ring(A_, r), [(ring(A4_, r % 2), wsc)], 1).then_inc(st["y"], 1)
            pipeline(pe, q.steps, [(3, yB), (2, trB)])
            finish(pe, "B")

            pe.wait_ge(*V.at("sDv"))

            def to_rows(o, source, name):
                for h in range(2):
                    ins = te.transpose(o[:, h * D:(h + 1) * D], source[:, h * HT:(h + 1) * HT], ident[:, :])
                PEQ.did(ins, name)

            def to_cols(o, name):
                for h in range(2):
                    ins = te.transpose(o[:, h * HT:(h + 1) * HT], sq_rows[1][:, h, :], ident[0:HT, 0:HT])
                PEQ.did(ins, name)
            to_rows(PS[0:HT, 0, :], sD, "sdv")
            pe.wait_ge(SPQ, 13)
            to_cols(PS[:, 1, :], "sdb")
            pe.wait_ge(*V.at("e"))
            to_rows(PS[0:HT, 2, :], sS, "ev")
            pe.wait_ge(SPQ, 25)
            to_cols(PS[:, 3, :], "mb")
            pe.wait_ge(*V.at("exa"))
            pe.wait_ge(*ACQ.at("exp"))
            sums("S1", lambda t_: onesf[:, 0:1], D + 1)

            q = ph["L1"]

            def trG(g, r):
                pe.wait_ge(*q.moved("ldg", g, r))
                if q.old(g, 1):
                    pe.wait_ge(*q.done("ev", g - 1))
                turn(wide(0), ring(G_, r), W).then_inc(st["tr"], 1)

            def y1(g, r):
                pe.wait_ge(*q.done("ev", g))
                pe.wait_ge(*q.moved("ldx", g, r))
                if q.old(g, 2):
                    pe.wait_ge(*q.done("apd", g - 2))
                    pe.wait_ge(*q.done("apa", g - 2))
                total(q, 2 + 2 * (r % 2), ring(X_, r), [(ring(A2_, r % 2), w1s)], None).then_inc(st["y"], 1)
            pipeline(pe, q.steps, [(0, trG), (0, y1)])
            finish(pe, "L1")

            def gated(name):
                q = ph[name]
                slot = name == "L3"
                n = 4 if slot else W
                XT, RN, Z, Y = gated_rings(slot)

                def ot(g, r):
                    pe.wait_ge(*q.done("w", g))
                    if slot:
                        if q.old(g, 1):
                            pe.wait_ge(*q.done("y", g - 1))
                        turn(PS[:, 3, :].rearrange("p (t d) -> p t d", d=D), XT(r), n).then_inc(st["ot"], 1)
                        return
                    if isinstance(g, int):
                        pe.wait_ge(*q.done("ev", min(g + 2, q.steps - 1)))
                    else:
                        pe.wait_ge(*q.done("ev", g + 2))
                    turn(wide(0), XT(r), n).then_inc(st["ot"], 1)

                def tr(g, r):
                    pe.wait_ge(*q.moved("ldx", g, r))
                    if q.old(g, 3):
                        pe.wait_ge(*q.done("y", g - 3))
                    if q.old(g, 1):
                        pe.wait_ge(*q.done("ev", g - 1))
                    turn(wide(0), ring(X_, r), n).then_inc(st["tr"], 1)

                def gates(h):
                    def f(g, r):
                        pe.wait_ge(*q.done("ev", g))
                        if q.old(g, 1):
                            pe.wait_ge(*q.done(f"sg{h}", g - 1))
                            pe.wait_ge(*q.done("tn", g - 1, h + 1))
                        for k in range(3):
                            ins = mm(PS[:, 2 + 3 * h + k, :], whT[:, k * D:(k + 1) * D],
                                     flat(XT(r))[:, 512 * h:512 * (h + 1)])
                        ins.then_inc(st[f"g{h}"], 1)
                    return f

                def slot_turns(g, r):
                    pe.wait_ge(*q.moved("ldx", g, r))
                    pe.wait_ge(*q.moved("ldg", g, r))
                    pe.wait_ge(*q.moved("ldc", g, r))
                    if q.old(g, 1):
                        pe.wait_ge(*q.done("ev", g - 1))
                    turn(PS[:, 0, :].rearrange("p (t d) -> p t d", d=D), ring(X_, r, 4), 4).then_inc(st["tr"], 1)
                    if q.old(g, 1):
                        pe.wait_ge(*q.done("eg", g - 1))
                    turn(PS[:, 1, :].rearrange("p (t d) -> p t d", d=D), ring(G_, r, 4), 4).then_inc(st["tg"], 1)
                    if q.old(g, 1):
                        pe.wait_ge(*q.done("ec", g - 1))
                    turn(PS[0:CNT, 2, :].rearrange("p (t d) -> p t d", d=D), cring(r), 4).then_inc(st["tc"], 1)

                def slot_gates(g, r):
                    for k in ("ev", "eg", "ec"):
                        pe.wait_ge(*q.done(k, g))
                    if q.old(g, 1):
                        pe.wait_ge(*q.done("sg0", g - 1))
                        pe.wait_ge(*q.done("tn", g - 1))
                    gt, ct = flat(ring(64, r % 2, 4)), flat(ring(20, r % 2, 4))[0:TYPES]
                    for k in range(3):
                        a = slice(k * D, (k + 1) * D)
                        mm(PS[:, 4 + k, :], whT[:, a], flat(XT(r)), True, k == 2)
                        b = 4 + k if k < 2 else 7
                        mm(PS[:, b, :], wcT[:, a], gt, k == 2, False)
                        ins = mm(PS[:, b, :], wcE[:, a], ct, False, True)
                    ins.then_inc(st["g0"], 1)
                if slot:
                    pipeline(pe, q.steps, [(3, ot), (1, slot_gates), (0, slot_turns)])
                else:
                    pipeline(pe, q.steps, [(3, ot), (1, gates(0)), (0, tr), (1, gates(1))])
                finish(pe, name)

            gated("C1")
            finish(pe, "G2")
            sums("S2")

            q = ph["L2"]

            def turns(g, r):
                pe.wait_ge(*q.done("u", g))
                if q.old(g, 1):
                    pe.wait_ge(*q.done("ev", g - 1))
                turn(wide(0), ring(A_, r % 2), W).then_inc(st["tr"], 1)
                pe.wait_ge(*q.moved("ldg", g, r))
                if q.old(g, 1):
                    pe.wait_ge(*q.done("eg", g - 1))
                turn(wide(6), ring(G_, r), W).then_inc(st["tg"], 1)

            def y2(g, r):
                pe.wait_ge(*q.done("ev", g))
                pe.wait_ge(*q.done("eg", g))
                if q.old(g, 2):
                    pe.wait_ge(*q.done("apd", g - 2))
                    pe.wait_ge(*q.done("apa", g - 2))
                total(q, 2 + 2 * (r % 2), ring(X_, r), [(ring(A2_, r % 2), wsc), (ring(A3_, r % 2), wnc)], 2)\
                    .then_inc(st["y"], 1)
            pipeline(pe, q.steps, [(1, turns), (2, y2)])
            finish(pe, "L2")
            gated("C2")
            finish(pe, "G3")
            sums("S3")
            gated("L3")

        @block.scalar
        def _(act):
            s = nc.scalar
            act.wait_ge(*V.at("wcx"))

            def root(q, name, after, out_, source):
                def f(g, r):
                    act.wait_ge(*q.done(after, g))
                    s.activation(out_[:, r, :], source(r), ACT.Sqrt, bias=epsc[:, :]).then_inc(st[name], 1)
                return f

            def apply_stage(q, source, first=BFWD, n=W, stored=True, scatters=False, extra=(), after="nm2"):
                def f(g, r):
                    act.wait_ge(*q.done(after, g))
                    if q.old(g):
                        if stored:
                            act.wait_ge(*q.moved("sto", g - R, r))
                        if scatters:
                            act.wait_ge(*q.moved("sct", g - R, r))
                        for k in extra:
                            act.wait_ge(*q.done(k, g - R))
                    for j in range(first, n):
                        ins = s.activation(ring(O_, r, n)[:, j, :], source(r)[:, j, :], ACT.Identity,
                                           bias=nm2[:, r, j:j + 1], scale=rs2[:, r, j:j + 1])
                    ins.then_inc(st["apa"], 1)
                return f

            def ybank(b0):
                return lambda r: wide(b0 + 2 * (r % 2))

            def copy(q, name, after, dest, source, reuse, n):
                def f(g, r):
                    act.wait_ge(*q.done(after, g))
                    if q.old(g, n):
                        act.wait_ge(*q.done(reuse, g - n))
                    s.activation(dest(r), source, ACT.Copy).then_inc(st[name], 1)
                return f

            def var(t):
                return lambda r: t[:, r, :, 1]

            def rows_by(dest, source, g, r, name):
                for j in range(W):
                    ins = s.activation(dest[:, j, :], source[:, j, :], ACT.Identity, bias=nm1[:, r, j:j + 1],
                                       scale=rs1[:, r, j:j + 1])
                ins.then_inc(st[name], 1)

            def first_layer(name):
                q = ph[name]
                slot = name == "L0"
                o = 1 if slot else 0
                rows_ = (lambda r: ring(A3_, r % 2)) if slot else (lambda r: ring(X_, r))

                def xn(g, r):
                    act.wait_ge(*q.done("nm1", g))
                    if q.old(g, 2):
                        act.wait_ge(*q.done("y", g - 2))
                    rows_by(ring(A_, r % 2), rows_(r), g, r, "xn")
                stages = [(1 + o, xn), (4 + o, apply_stage(q, ybank(0), scatters=slot, extra=("sdp",) if slot else ())),
                          (o, root(q, "sq1", "ag1", sd1, var(mv1))), (3 + o, root(q, "sq2", "ag2", sd2, var(mv2)))]
                if slot:
                    stages = [(0, copy(q, "ev", "tr", lambda r: ring(A2_, r % 2), wide(4), "h", 2))] + stages
                pipeline(act, q.steps, stages)
                finish(act, name)

            def sums(name, width=D):
                q = ph[name]

                def one(g, r):
                    if q.old(g):
                        if "sto" in q.dmas:
                            act.wait_ge(*q.moved("sto", g - R, r))
                        if "qq" in q.mult:
                            act.wait_ge(*q.done("qq", g - R))
                    for j in range(4):
                        act.wait_ge(*q.done("sm", g, j + 1))
                        s.activation(osum(r)[:, j, 0:width], PS[:, j % 2, 0:width], ACT.Copy).then_inc(st["cv"], 1)
                pipeline(act, q.steps, [(0, one)])
                finish(act, name)

            first_layer("A")
            sums("S0", D + CNT)
            first_layer("L0")

            q = ph["B"]

            def x2(g, r):
                act.wait_ge(*q.done("nm1", g))
                if q.old(g):
                    act.wait_ge(*q.moved("st2", g - R, r))
                    act.wait_ge(*q.done("y", g - R))
                rows_by(ring(A_, r), ring(X_, r), g, r, "xn")
            pipeline(act, q.steps, [
                (3, copy(q, "ev", "tr", lambda r: ring(A4_, r % 2), wide(0), "y", 2)),
                (1, x2),
                (5, apply_stage(q, ybank(2))),
                (0, root(q, "sq1", "ag1", sd1, var(mv1))),
                (1, root(q, "sq3", "q", sd3, lambda r: rs3[:, r, :])),
                (4, root(q, "sq2", "ag2", sd2, var(mv2)))])
            finish(act, "B")
            act.wait_ge(*V.at("exa"))
            ACQ.did(s.activation(ew[:, :], ew[:, :], ACT.Exp), "exp")
            act.wait_ge(*ACQ.at("exp"))
            sums("S1", D + 1)
            q = ph["L1"]
            pipeline(act, q.steps, [
                (0, copy(q, "ev", "tr", lambda r: ring(A2_, r % 2), wide(0), "y", 2)),
                (2, apply_stage(q, ybank(2), scatters=True)),
                (1, root(q, "sq2", "ag2", sd2, var(mv2)))])
            finish(act, "L1")

            def gated(name):
                q = ph[name]
                slot = name == "L3"
                n = 4 if slot else W
                XT, RN, Z, Y = gated_rings(slot)

                def th(g, r):
                    act.wait_ge(*q.done("tn", g))
                    s.activation(flat(RN(r)), flat(RN(r)), ACT.Tanh, bias=c(BIH + 2)).then_inc(st["th"], 1)

                def sg(h):
                    def f(g, r):
                        act.wait_ge(*q.done(f"g{h}", g))
                        if q.old(g, 2):
                            act.wait_ge(*q.done("w", g - 2))
                        b = 4 if slot else 2 + 3 * h
                        a = slice(512 * h, 512 * (h + 1))
                        s.activation(flat(RN(r))[:, a], PS[:, b, :], ACT.Sigmoid, bias=c(BR))
                        s.activation(flat(Z(r))[:, a], PS[:, b + 1, :], ACT.Sigmoid, bias=c(BZ)).then_inc(st[f"sg{h}"], 1)
                    return f
                last_ = apply_stage(q, Y, 0, n, stored=not slot, scatters=slot, after="nw")
                if slot:
                    pipeline(act, q.steps, [
                        (5, last_), (2, th), (1, sg(0)),
                        (0, copy(q, "ev", "tr", lambda r: flat(XT(r)), PS[:, 0, :], "ot", R)),
                        (0, copy(q, "eg", "tg", lambda r: flat(ring(64, r % 2, 4)), PS[:, 1, :], "g0", 2)),
                        (0, copy(q, "ec", "tc", lambda r: flat(ring(20, r % 2, 4))[0:CNT], PS[0:CNT, 2, :], "g0", 2))])
                else:
                    pipeline(act, q.steps, [
                        (5, last_), (2, th), (1, sg(0)),
                        (0, copy(q, "ev", "tr", lambda r: XT(r), wide(0), "ot", R)),
                        (1, sg(1))])
                finish(act, name)

            gated("C1")
            act.wait_ge(*V.at("rv"))
            ACQ.did(s.activation(ew[:, :], sD[:, :], ACT.Sqrt), "rv")
            sums("S2")
            q = ph["L2"]

            def u2(g, r):
                act.wait_ge(*q.done("nm1", g))
                if q.old(g, 2):
                    act.wait_ge(*q.done("tr", g - 2))
                rows_by(ring(A_, r % 2), ring(X_, r), g, r, "u")
            pipeline(act, q.steps, [
                (1, u2),
                (1, copy(q, "ev", "tr", lambda r: ring(A2_, r % 2), wide(0), "y", 2)),
                (1, copy(q, "eg", "tg", lambda r: ring(A3_, r % 2), wide(6), "y", 2)),
                (4, apply_stage(q, ybank(2), scatters=True)),
                (0, root(q, "sq1", "ag1", sd1, var(mv1))),
                (3, root(q, "sq2", "ag2", sd2, var(mv2)))])
            finish(act, "L2")
            gated("C2")
            sums("S3")
            gated("L3")


_INS = ["x", "src", "dst", "edge_type_9", "L0_gnn_W", "L0_gnn_gamma", "L0_gnn_beta", "L1_gnn_W", "L1_gnn_attn_w",
        "L2_gnn_gamma", "L2_gnn_beta", "L2_gnn_W_self", "L2_gnn_W_neigh", "L2_gnn_b", "L3_gnn_W_msg", "L3_gnn_b_msg",
        "L3_gnn_edge_embed", "L3_gnn_W_ih", "L3_gnn_W_hh", "L3_gnn_b_ih", "L3_gnn_b_hh"]


def kernel(**inputs):
    import numpy as _np
    import concourse.bacc as _bacc
    from concourse import mybir as _mybir
    from concourse.bass_utils import run_bass_kernel_spmd as _run
    nc = _bacc.Bacc("TRN2", target_bir_lowering=False, num_devices=1)
    arrays, args = {}, []
    for name in _INS:
        a = _np.ascontiguousarray(inputs[name])
        arrays[f"in_{name}_dram"] = a
        args.append(nc.dram_tensor(f"in_{name}_dram", a.shape, _mybir.dt.from_np(a.dtype), kind="ExternalInput").ap())
    shape = inputs["x"].shape
    args.append(nc.dram_tensor("out_0_dram", shape, _mybir.dt.float32, kind="ExternalOutput").ap())
    gnn_program(nc, *args)
    r = _run(nc, [arrays], core_ids=[0])
    return r.results[0]["out_0_dram"]
```

```python
from contextlib import ExitStack

import concourse.bass as bass
from concourse import mybir

F32 = mybir.dt.float32
I32 = mybir.dt.int32
BF16 = mybir.dt.bfloat16
ALU = mybir.AluOpType
ACT = mybir.ActivationFunctionType
AX = mybir.AxisListType.X
DS = bass.ds

P = 128
D = 128
EPS = 1e-5
SLOPE = 0.01
NEG = 1e30
MAGIC = 1597463007.0
TYPES = 9
CNT = TYPES + 1
R = 4


class Phase:

    def __init__(self, steps, stages, rings, st, rg, base):
        self.steps, self.st, self.rg = steps, st, rg
        self.mult, self.dmas = dict(stages), dict(rings)
        self.base = {k: base.get(k, 0) for k in list(self.mult) + [(k, r) for k in self.dmas for r in range(R)]}
        for k, m in self.mult.items():
            base[k] = base.get(k, 0) + m * steps
        for k, m in self.dmas.items():
            for r in range(R):
                base[(k, r)] = base.get((k, r), 0) + 16 * m * len(range(r, steps, R))
        self.end = {k: base[k] for k in self.base}

    def done(self, name, g, k=None):
        m = self.mult[name]
        return self.st[name], g * m + (self.base[name] + (m if k is None else k))

    def moved(self, name, g, r):
        m = self.dmas[name]
        return self.rg[name][r], (g - r) * (16 * m // R) + (self.base[(name, r)] + 16 * m)

    def old(self, g, n=R):
        return not isinstance(g, int) or g >= n


class Steps:

    def __init__(self, sem, names):
        self.sem, self.names, self.k = sem, names.split(), 0

    def did(self, ins, name):
        assert self.names[self.k] == name, (self.names[self.k], name)
        self.k += 1
        ins.then_inc(self.sem, 1)

    def at(self, name):
        return self.sem, self.names.index(name) + 1


def pipeline(eng, steps, stages):
    lag = max(o for o, _ in stages)
    lo, hi = -(-(lag + R) // R) * R, steps // R * R
    for i in range(lo):
        for o, body in stages:
            if 0 <= i - o < steps:
                body(i - o, (i - o) % R)
    if hi > lo:
        with eng.Fori(lo // R, hi // R) as block:
            for k in range(R):
                for o, body in stages:
                    body(block * R + (k - o), (k - o) % R)
    for i in range(max(hi, lo), steps + lag):
        for o, body in stages:
            if 0 <= i - o < steps:
                body(i - o, (i - o) % R)


def gnn_program(nc, x, src, dst, etype, w0, gamma0, beta0, w1, attn, gamma2, beta2, w_self, w_neigh, b2,
                w_msg, b_msg, embed, w_ih, w_hh, b_ih, b_hh, out):
    N, E = x.shape[0], src.shape[0]
    T = -(-E // (8 * P)) * 8
    HT = T // 2
    NS = P * T
    BIG = 1 << 20
    W = 8
    BLK = W * P
    ND = -(-N // BLK)
    TAILP = (N - (ND - 1) * BLK) // W
    assert TAILP * W == N - (ND - 1) * BLK and T == 200
    C1N = ND // 2
    GS = T // 4

    ctx = ExitStack()
    with ctx:
        def sb(name, shape, dt=F32):
            return ctx.enter_context(nc.sbuf_tensor(name, shape, dt))

        def sem(name):
            return ctx.enter_context(nc.semaphore(name))

        tab = [x] + [nc.dram_tensor(f"t{k}", [N, D], F32) for k in (1, 2, 3)]
        xs = [nc.dram_tensor(f"xs{k}", [NS, D], F32) for k in range(4)]
        agg_d = nc.dram_tensor("agg_d", [NS, D], F32)
        cnt_d = nc.dram_tensor("cnt_d", [NS, CNT], F32)
        dst_d = nc.dram_tensor("dst_d", [NS], F32)
        seq_d = nc.dram_tensor("seq_d", [NS], F32)
        seq2_d = nc.dram_tensor("seq2_d", [NS], F32)
        row_d = nc.dram_tensor("row_d", [P], F32)
        row2_d = nc.dram_tensor("row2_d", [P], F32)

        def slots(t):
            return t.rearrange("(p t) d -> p t d", p=P)

        def nodes(t, g):
            if isinstance(g, int):
                return t[g * BLK:min(N, (g + 1) * BLK), :].rearrange("(p t) d -> p t d", t=W)
            return t[DS(g * BLK, BLK), :].rearrange("(p t) d -> p t d", t=W)

        def tiles(t, g, n):
            if isinstance(g, int):
                return t[:, g * n:(g + 1) * n]
            return t[:, DS(g * n, n)]

        S = sb("S", [P, T, D + 1])
        BUF = sb("BUF", [P, 144, D])
        gring = sb("gring", [P, R, 4, D])
        iring = sb("iring", [P, R, 4], I32)
        oring = sb("oring", [P, R, 8], I32)
        srci, dgi, sci = sb("srci", [P, T], I32), sb("dgi", [P, T], I32), sb("sci", [P, T], I32)
        dstc = sb("dstc", [P, T])
        dprev = sb("dprev", [P, T])
        lastc = sb("lastc", [P, T])
        typec = sb("typec", [P, T])
        rdeg, sS, sD, ew, mx = sb("rdeg", [P, T]), sb("sS", [P, T]), sb("sD", [P, T]), sb("ew", [P, T]), sb("mx", [P, T])
        col = sb("col", [P, 32])
        row = sb("row", [1, 8, P])
        ident, onesf, cen = sb("ident", [P, P]), sb("onesf", [P, P]), sb("cen", [P, P])
        e127 = sb("e127", [P, 1])
        gam_b = sb("gam_b", [P, D])
        wa_b = sb("wa_b", [P, 2, D])
        ones3, bias3 = sb("ones3", [3, P], BF16), sb("bias3", [3, 3, D], BF16)
        w0T, w1s, wsc, wnc = sb("w0T", [P, D]), sb("w1s", [P, D]), sb("wsc", [P, D]), sb("wnc", [P, D])
        whT, wcT = sb("whT", [P, 3 * D]), sb("wcT", [P, 3 * D])
        wcE = sb("wcE", [TYPES, 3 * D])
        st1, st2 = sb("st1", [P, W, 6]), sb("st2", [P, W, 6])
        mv1, mv2 = sb("mv1", [P, R, W, 2]), sb("mv2", [P, R, W, 2])
        sd1, sd2, sd3 = sb("sd1", [P, R, W]), sb("sd2", [P, R, W]), sb("sd3", [P, R, W])
        rs1, rs2, rs3 = sb("rs1", [P, R, W]), sb("rs2", [P, R, W]), sb("rs3", [P, R, W])
        nm1, nm2 = sb("nm1", [P, R, W]), sb("nm2", [P, R, W])
        nwt, nwi = sb("nwt", [P, 2, W]), sb("nwi", [P, W], I32)
        epsc = sb("epsc", [P, 1])

        PS = ctx.enter_context(nc.psum_tensor("PS", [P, 8, 512], F32))

        def wide(b):
            return PS[:, b:b + 2, :].rearrange("p b (t d) -> p (b t) d", d=D)

        def ring(first, r, w=W):
            return BUF[:, first + r * w:first + (r + 1) * w, :]

        def bank_of(r, j):
            return 4 * (r % 2) + j

        def flat(t):
            return t.rearrange("p a b -> p (a b)")

        def c(k, n=1):
            return col[:, k:k + n]

        G2, B2, BM, A1, A2, BIH, BHH, BR, BZ, CC = 0, 1, 2, 3, 4, 5, 8, 11, 12, 13

        st = {k: sem("s_" + k) for k in (
            "bn1 ag1 sq1 rc1 nm1 xn gm y bn2 ag2 sq2 rc2 nm2 ya apa tr ev h mm rel q r3 sq3 u tg eg tc ec "
            "g0 g1 sg0 sg1 th ot tn w nw ix so mk sm cv qq sdp").split()}
        rg = {k: [sem(f"{k}{r}") for r in range(R)] for k in "ldx ldg ldc sto st2 gat plc sct".split()}
        loaded, bounce = sem("loaded"), sem("bounce")
        pool_pass = sem("pool_pass")
        V = Steps(sem("dve_steps"),
                  "idf idx cen embc parts wcx oh sDv seqv e seqe exa rv")
        PEQ = Steps(sem("pe_steps"), "ids emb wcx sdv sdb ev mb")
        ACQ = Steps(sem("act_steps"), "exp rv")
        POOL = Steps(sem("pool_steps"), "consts ident")
        SEQ = Steps(sem("scan_steps"), "a0 a2 a5 b0 b2 c0 c2 c5")
        SPQ = sem("sp_steps")

        base = {}

        def phase(steps, stages, rings):
            return Phase(steps, [(s.split(":")[0], int((s.split(":") + ["1"])[1])) for s in stages.split()],
                         [(s.split(":")[0], int((s.split(":") + ["1"])[1])) for s in rings.split()], st, rg, base)

        GATHER, SUM = "gat:4 plc", "mk sm:4 cv:4"
        LN1, LN2 = "bn1 ag1 sq1 rc1 nm1", "ya bn2 ag2 sq2 rc2 nm2 apa"
        CS = "tr ev g0 g1 sg0 sg1 th ot tn:2 w:3 y bn2 ag2 nw:13 apa"
        ph = {}
        ph["G0"] = phase(GS, "ix", GATHER)
        ph["GD"] = phase(GS, "ix", GATHER)
        ph["A"] = phase(ND, LN1 + " xn gm y " + LN2, "ldx sto")
        ph["S0"] = phase(GS, SUM + " qq", "ldg sto:2")
        ph["L0"] = phase(T // W, LN1 + " xn gm y " + LN2 + " tr ev h rel sdp:2 so", "ldx ldg sto sct:8")
        ph["G1"] = phase(GS, "ix", GATHER)
        ph["B"] = phase(ND, LN1 + " xn q:2 sq3 r3 u tr ev y " + LN2, "ldx sto st2")
        ph["S1"] = phase(GS, SUM + " qq:3", "ldg sto")
        ph["L1"] = phase(T // W, "tr ev y so " + LN2, "ldx ldg sto sct:8")
        ph["G2"] = phase(GS, "ix", GATHER)
        ph["C1"] = phase(C1N, CS, "ldx sto")
        ph["S2"] = phase(GS, SUM + " qq", "ldg sto")
        ph["L2"] = phase(T // W, LN1 + " u tr ev tg eg y so " + LN2, "ldx ldg sto sct:8")
        ph["G3"] = phase(GS, "ix", GATHER)
        ph["C2"] = phase(ND - C1N, CS, "ldx sto")
        ph["S3"] = phase(GS, SUM, "ldg sto")
        ph["L3"] = phase(GS, "tr tg tc ev eg ec g0 sg0 th ot tn:2 w:3 y bn2 ag2 nw:13 apa so", "ldx ldg ldc sct:4")

        def finish(eng, name, but=()):
            q = ph[name]
            for k, n in q.end.items():
                if k in but or (isinstance(k, tuple) and k[0] in but):
                    continue
                eng.wait_ge(rg[k[0]][k[1]] if isinstance(k, tuple) else st[k], n)

        def begins_after(eng, *names):
            for n in names:
                finish(eng, n)

        X_, O_, A_ = 0, 32, 64
        A2_, A3_, A4_ = 80, 96, 112
        G_ = 112
        MM_, MC_, DB_, OB_, QB_, MX_ = 0, 16, 32, 48, 72, 88

        def osum(r):
            return flat(BUF[:, OB_:OB_ + 24, :])[:, r * 4 * (D + CNT):(r + 1) * 4 * (D + CNT)].rearrange(
                "p (t d) -> p t d", d=D + CNT)

        def cring(r):
            return flat(BUF[:, 16:18, :])[:, r * 4 * CNT:(r + 1) * 4 * CNT].rearrange("p (t k) -> p t k", k=CNT)

        oh = flat(BUF[:, 96:112, :])[:, 0:T * CNT].rearrange("p (t k) -> p t k", k=CNT)

        def raw(k, n=1):
            return BUF[:, k:k + n, :]
        RI = flat(BUF[:, 0:8, :]).bitcast(I32).rearrange("p (q h d) -> p q h d", h=2, d=D)
        RF = flat(BUF[:, 8:20, :]).rearrange("p (q h d) -> p q h d", h=2, d=D)
        R_W0, R_W1, R_WS, R_WN, R_WM, R_WIH, R_WHH, R_EMB, R_W1T, R_WIHT, R_EMBT, R_AA, R_GWS, R_GWN = (
            20, 21, 22, 23, 24, 25, 28, 31, 32, 33, 36, 37, 39, 40)

        parts = flat(BUF[0:1, 44:49, :]).bitcast(BF16)[:, 0:9 * D].rearrange("p (k w d) -> p k w d", k=3, w=3)
        part_f = BUF[0:1, 49:52, :]
        bias_r = BUF[0:1, 52:55, :]

        def scr(k):
            return flat(BUF[:, 112 + 2 * k:114 + 2 * k, :])[:, 0:T]
        dP, penF, penB, va, vb, vc = scr(0), scr(1), scr(2), scr(3), scr(4), scr(5)
        sq_rows = [BUF[0:HT, 124:126, :], BUF[0:HT, 126:128, :]]

        def seq(t):
            return t.rearrange("(h p d) -> p h d", h=2, d=D)

        def seqp(t):
            return t.rearrange("(p t) -> p t", p=P)

        block = ctx.enter_context(nc.Block())

        @block.sync
        def _(sp):
            sp.wait_ge(*POOL.at("consts"))

            def ids(k, v, a0):
                n = E - a0
                full = n // D
                sp.dma_start(RI[0:HT, k, 0, :], v[a0:a0 + HT * D].rearrange("(p d) -> p d", d=D)).then_inc(loaded, 16)
                sp.dma_start(RI[0:full - HT, k, 1, :],
                             v[a0 + HT * D:a0 + full * D].rearrange("(p d) -> p d", d=D)).then_inc(loaded, 16)
                sp.dma_start(RI[full - HT:full - HT + 1, k, 1, 0:n - full * D],
                             v[a0 + full * D:E].rearrange("(p d) -> p d", p=1)).then_inc(loaded, 16)
            ids(0, dst, 0)
            ids(1, dst, 1)
            ids(2, src, 0)
            ids(3, etype, 0)
            with nc.allow_non_contiguous_dma(reason="biases as columns"):
                for k, v in ((G2, gamma2), (B2, beta2), (BM, b_msg), (A1, attn[0:D]), (A2, attn[D:2 * D])):
                    sp.dma_start(c(k), v.rearrange("(p o) -> p o", o=1)).then_inc(loaded, 16)
                sp.dma_start(c(BIH, 3), b_ih.rearrange("(c p) -> p c", p=D)).then_inc(loaded, 16)
                sp.dma_start(c(BHH, 3), b_hh.rearrange("(c p) -> p c", p=D)).then_inc(loaded, 16)
            for k, w in ((R_W0, w0), (R_W1, w1), (R_WS, w_self), (R_WN, w_neigh), (R_WM, w_msg)):
                sp.dma_start(raw(k)[:, 0, :], w).then_inc(loaded, 16)
            sp.dma_start(w1s[:, :], w1).then_inc(loaded, 16)
            sp.dma_start(raw(R_WIH, 3), w_ih.rearrange("(c p) f -> p c f", p=D)).then_inc(loaded, 16)
            sp.dma_start(raw(R_WHH, 3), w_hh.rearrange("(c p) f -> p c f", p=D)).then_inc(loaded, 16)
            sp.dma_start(raw(R_EMB)[0:TYPES, 0, :], embed).then_inc(loaded, 16)
            sp.dma_start(bias_r[:, 0, :], beta0.rearrange("(o f) -> o f", o=1)).then_inc(loaded, 16)
            sp.dma_start(row[:, 0, :], b2.rearrange("(o f) -> o f", o=1)).then_inc(loaded, 16)
            sp.dma_start(gam_b[:, :], gamma0.rearrange("(o f) -> o f", o=1).to_broadcast([P, D])).then_inc(loaded, 16)
            sp.wait_ge(*V.at("idf"))
            sp.dma_start(seq(dst_d), RF[0:HT, 0, :, :]).then_inc(bounce, 16)
            sp.wait_ge(bounce, 16)
            sp.wait_ge(*V.at("parts"))
            for k in range(3):
                sp.dma_start(bias3[k:k + 1, :, :], parts[:, k, :, :]).then_inc(bounce, 16)
            sp.wait_ge(bounce, 64)

            sp_pass = sem("sp_pass")

            def hold():
                sp.sem_inc(sp_pass, 1)

            def dense(name, load, store, lag):
                pipeline(sp, ph[name].steps, [(0, load), (lag, store)])

            def load_x(q, g, r, source, freed, first=X_):
                if q.old(g):
                    for k in freed:
                        sp.wait_ge(*q.done(k, g - R))
                        hold()
                ap = ring(first, r)
                if isinstance(g, int) and source.shape[0] < P:
                    ap = ap[0:source.shape[0]]
                sp.dma_start(ap, source).then_inc(rg["ldx"][r], 16)

            def store_nodes(q, g, r, table, first=O_, key="sto"):
                ap, dest = ring(first, r), table
                if dest.shape[0] < P:
                    ap = ap[0:dest.shape[0]]
                sp.dma_start(dest, ap).then_inc(rg[key][r], 16)

            sp.wait_ge(*V.at("wcx"))
            q = ph["A"]

            def load(g, r):
                load_x(q, g, r, nodes(x, g), ("xn", "y"))

            def store(g, r):
                sp.wait_ge(*q.done("apa", g))
                hold()
                store_nodes(q, g, r, nodes(tab[1], g))
            dense("A", load, store, 6)

            def sums(name):
                q = ph[name]

                def load(g, r):
                    if q.old(g):
                        sp.wait_ge(*q.done("mk", g - R))
                        hold()
                    ids = dst_d[DS(g * 4 * D, 4 * D)] if not isinstance(g, int) else dst_d[g * 4 * D:(g + 1) * 4 * D]
                    sp.dma_start(flat(ring(DB_, r, 4)), ids.rearrange("(o f) -> o f", o=1).to_broadcast([P, 4 * D]))\
                        .then_inc(rg["ldg"][r], 16)

                def store(g, r):
                    if name in ("S1", "S2"):
                        sp.wait_ge(*q.done("qq", g))
                        hold()
                        sp.dma_start(tiles(slots(agg_d), g, 4), ring(QB_, r, 4)).then_inc(rg["sto"][r], 16)
                    else:
                        sp.wait_ge(*q.done("cv", g))
                        hold()
                        sp.dma_start(tiles(slots(agg_d), g, 4), osum(r)[:, :, 0:D]).then_inc(rg["sto"][r], 16)
                        if name == "S0":
                            sp.dma_start(tiles(slots(cnt_d), g, 4), osum(r)[:, :, D:]).then_inc(rg["sto"][r], 16)
                pipeline(sp, q.steps, [(0, load), (4, store)])
                finish(sp, name)

            def slot_phase(name, k, freed_x, freed_g, done, lag, w=W):
                q = ph[name]

                def load(g, r):
                    load_x(q, g, r, tiles(slots(xs[k]), g, W), freed_x)
                    if q.old(g):
                        for n in freed_g:
                            sp.wait_ge(*q.done(n, g - R))
                            hold()
                    sp.dma_start(ring(G_, r, W), tiles(slots(agg_d), g, W))\
                        .then_inc(rg["ldg"][r], 16)

                def store(g, r):
                    for n in done:
                        sp.wait_ge(*q.done(n, g))
                        hold()
                    sp.dma_start(tiles(slots(xs[k + 1]), g, W), ring(O_, r)).then_inc(rg["sto"][r], 16)
                pipeline(sp, q.steps, [(0, load), (lag, store)])
                finish(sp, name)

            finish(sp, "A")
            sums("S0")
            finish(sp, "GD")
            slot_phase("L0", 0, ("y", "rel"), ("tr",), ("apa",), 7)

            q = ph["B"]

            def load(g, r):
                load_x(q, g, r, nodes(tab[1], g), ("bn1", "xn"))

            def store2(g, r):
                sp.wait_ge(*q.done("xn", g))
                hold()
                store_nodes(q, g, r, nodes(tab[2], g), A_, "st2")

            def store3(g, r):
                sp.wait_ge(*q.done("apa", g))
                hold()
                store_nodes(q, g, r, nodes(tab[3], g))
            pipeline(sp, q.steps, [(0, load), (3, store2), (7, store3)])
            finish(sp, "B")

            n = 64

            def bring(dest, source, *wait):
                nonlocal n
                for w in wait:
                    sp.wait_ge(*w)
                sp.dma_start(dest, source).then_inc(bounce, 16)
                n += 16
                sp.wait_ge(bounce, n)
                sp.sem_inc(SPQ, 1)

            with nc.allow_non_contiguous_dma(reason="a column of 128 values"):
                def across(tag):
                    bring(row_d[:], vb[:, T - 1:T] if tag == "b" else vb[:, 0:1], SEQ.at(f"{tag}0"))
                    bring(row[:, 1, :], row_d[:].rearrange("(o f) -> o f", o=1))
                    bring(row2_d[:], row[:, 3, :], SEQ.at(f"{tag}2"))
                    bring(c(CC), row2_d[:].rearrange("(p o) -> p o", o=1))

                bring(dP, seqp(dst_d))
                bring(row_d[:], dP[:, 0:1])
                bring(row[:, 4, :], row_d[:].rearrange("(o f) -> o f", o=1))
                bring(row2_d[:], dP[:, T - 1:T])
                bring(row[:, 5, :], row2_d[:].rearrange("(o f) -> o f", o=1))
                bring(seq(seq_d), sq_rows[0], V.at("seqv"))
                bring(va, seqp(seq_d))
                across("a")
                bring(seqp(seq2_d), vc, SEQ.at("a5"))
                bring(sq_rows[1], seq(seq2_d))
                bring(seq(seq_d), sq_rows[0], V.at("seqe"))
                bring(va, seqp(seq_d))
                across("b")
                across("c")
                bring(seqp(seq2_d), vc, SEQ.at("c5"))
                bring(sq_rows[1], seq(seq2_d))

            sums("S1")
            slot_phase("L1", 1, ("ya",), ("tr",), ("apa",), 4)

            def last_layer(name, g0):
                q = ph[name]

                def load(g, r):
                    load_x(q, g, r, nodes(tab[3], g + g0), ("y",))

                def store(g, r):
                    sp.wait_ge(*q.done("apa", g))
                    hold()
                    store_nodes(q, g, r, nodes(out, g + g0))
                dense(name, load, store, 7)
                finish(sp, name)

            last_layer("C1", 0)
            sums("S2")
            slot_phase("L2", 2, ("ya", "u"), ("tg",), ("apa",), 6)
            last_layer("C2", C1N)
            sums("S3")

            q = ph["L3"]

            def load(g, r):
                if q.old(g):
                    sp.wait_ge(*q.done("y", g - R))
                    hold()
                sp.dma_start(ring(X_, r, 4), tiles(slots(xs[3]), g, 4)).then_inc(rg["ldx"][r], 16)
                if q.old(g):
                    sp.wait_ge(*q.done("tg", g - R))
                    hold()
                sp.dma_start(ring(G_, r, 4), tiles(slots(agg_d), g, 4)).then_inc(rg["ldg"][r], 16)
                if q.old(g):
                    sp.wait_ge(*q.done("tc", g - R))
                    hold()
                sp.dma_start(cring(r), tiles(slots(cnt_d), g, 4)).then_inc(rg["ldc"][r], 16)
            pipeline(sp, q.steps, [(0, load)])
            finish(sp, "L3")

        @block.gpsimd
        def _(pool):
            g_ = nc.gpsimd

            def hold():
                pool.sem_inc(pool_pass, 1)

            g_.memset(flat(BUF[:, 0:2, :]).bitcast(I32), -5)
            g_.memset(flat(BUF[:, 2:4, :]).bitcast(I32), -5)
            g_.memset(flat(BUF[:, 4:8, :]).bitcast(I32), 0)
            g_.memset(epsc[:, :], EPS)
            g_.memset(onesf[:, :], 1.0)
            g_.memset(ident[:, :], 0.0)
            POOL.did(g_.memset(e127[:, :], 0.0), "consts")
            pool.wait_ge(*POOL.at("consts"))
            g_.affine_select(out=e127[:, :], in_=e127[:, :], compare_op=ALU.not_equal, fill=1.0, base=-(P - 1),
                             pattern=[[0, 1]], channel_multiplier=1)
            POOL.did(g_.affine_select(out=ident[:, :], in_=ident[:, :], compare_op=ALU.not_equal, fill=1.0, base=0,
                                      pattern=[[-1, P]], channel_multiplier=1), "ident")

            def gather(name, index, table, dest):
                q = ph[name]

                def fetch(g, r):
                    if q.old(g):
                        pool.wait_ge(*q.moved("plc", g - R, r))
                        hold()
                    g_.tensor_copy(iring[:, r, :], tiles(index, g, 4)).then_inc(st["ix"], 1)
                    pool.wait_ge(*q.done("ix", g))
                    hold()
                    for j in range(4):
                        g_.indirect_dma_start(out=gring[:, r, j, :], out_offset=None, in_=table[:, :],
                                              in_offset=bass.IndirectOffsetOnAxis(ap=iring[:, r, j:j + 1], axis=0))\
                            .then_inc(rg["gat"][r], 16)

                def place(g, r):
                    pool.wait_ge(*q.moved("gat", g, r))
                    hold()
                    g_.dma_start(tiles(dest, g, 4), gring[:, r, :, :]).then_inc(rg["plc"][r], 16)
                pipeline(pool, q.steps, [(0, fetch), (2, place)])
                finish(pool, name, ("ix",))
                hold()

            def scatter(name, table, n, done, lag):
                q = ph[name]

                def put(g, r):
                    if q.old(g):
                        pool.wait_ge(*q.moved("sct", g - R, r))
                        hold()
                    g_.tensor_copy(oring[:, r, 0:n], tiles(sci, g, n)).then_inc(st["so"], 1)
                    pool.wait_ge(*q.done("so", g))
                    hold()
                    for k in done:
                        pool.wait_ge(*q.done(k, g))
                        hold()
                    for j in range(n):
                        g_.indirect_dma_start(out=table[:, :],
                                              out_offset=bass.IndirectOffsetOnAxis(ap=oring[:, r, j:j + 1], axis=0),
                                              in_=ring(O_, r, n)[:, j, :], in_offset=None,
                                              bounds_check=N - 1, oob_is_err=False).then_inc(rg["sct"][r], 16)
                pipeline(pool, q.steps, [(0, put)])
                finish(pool, name)
                hold()

            pool.wait_ge(*V.at("idx"))
            gather("G0", srci, x, S[:, :, 0:D])
            gather("GD", dgi, x, slots(xs[0]))
            finish(pool, "A")
            scatter("L0", tab[1], 8, ("apa",), 4)
            gather("G1", srci, tab[1], S[:, :, 0:D])
            finish(pool, "B")
            scatter("L1", tab[2], 8, ("apa",), 3)
            gather("G2", srci, tab[2], S[:, :, 0:D])
            finish(pool, "C1")
            scatter("L2", tab[3], 8, ("apa",), 4)
            gather("G3", srci, tab[3], S[:, :, 0:D])
            finish(pool, "C2")
            scatter("L3", out, 4, ("apa",), 0)

        def gated_rings(slot):
            if slot:
                return (lambda r: ring(48, r, 4), lambda r: ring(72, r % 2, 4), lambda r: ring(80, r % 2, 4),
                        lambda r: ring(96, r % 2, 4))
            return (lambda r: ring(64, r), lambda r: ring(112, r % 2), lambda r: ring(128, r % 2),
                    lambda r: ring(96, r % 2))

        @block.vector
        def _(dve):
            v = nc.vector
            own = sem("dve_own")
            dpass = sem("dve_pass")
            cnt = 0

            def hold():
                dve.sem_inc(dpass, 1)

            def do(ins):
                nonlocal cnt
                ins.then_inc(own, 1)
                cnt += 1
                dve.wait_ge(own, cnt)

            def step(ins, name, steps=V):
                steps.did(ins, name)
                dve.wait_ge(*steps.at(name))

            dve.wait_ge(loaded, 16 * 31)
            do(v.tensor_copy(RF[0:HT, 0:4], RI[0:HT, 0:4]))
            do(v.tensor_tensor(RF[0:HT, 4], RF[0:HT, 0], RF[0:HT, 1], ALU.not_equal))
            do(v.scalar_tensor_tensor(RF[0:HT, 5], RF[0:HT, 0], float(-BIG), RF[0:HT, 4], ALU.add, ALU.mult))
            step(v.tensor_scalar(RF[0:HT, 5], RF[0:HT, 5], float(BIG), None, ALU.add), "idf")
            dve.wait_ge(*PEQ.at("ids"))
            do(v.tensor_copy(dstc[:, :], PS[:, 0, 0:T]))
            do(v.tensor_copy(srci[:, :], PS[:, 2, 0:T]))
            do(v.tensor_scalar(typec[:, :], PS[:, 3, 0:T], 0.0, float(TYPES - 1), ALU.max, ALU.min))
            do(v.tensor_copy(lastc[:, :], PS[:, 4, 0:T]))
            do(v.tensor_copy(sci[:, :], PS[:, 5, 0:T]))
            step(v.tensor_scalar(dgi[:, :], dstc[:, :], 0.0, None, ALU.max), "idx")
            dve.wait_ge(*POOL.at("ident"))
            do(v.memset(dprev[:, :], -1.0))
            do(v.tensor_scalar(dprev[:, 1:T], dstc[:, 0:T - 1], 1.0, e127[:, 0:1], ALU.add, ALU.mult))
            do(v.tensor_scalar(dprev[:, 1:T], dprev[:, 1:T], -1.0, None, ALU.add))
            do(v.tensor_scalar(cen[:, :], ident[:, :], -1.0 / D, None, ALU.add))
            do(v.tensor_scalar(raw(R_AA)[:, 0, :], onesf[:, :], c(A1), None, ALU.mult))
            do(v.tensor_scalar(raw(R_AA + 1)[:, 0, :], onesf[:, :], c(A2), None, ALU.mult))
            do(v.tensor_scalar(raw(R_GWS)[:, 0, :], raw(R_WS)[:, 0, :], c(G2), None, ALU.mult))
            do(v.tensor_scalar(raw(R_GWN)[:, 0, :], raw(R_WN)[:, 0, :], c(G2), None, ALU.mult))
            do(v.tensor_tensor(c(BR), c(BIH), c(BHH), ALU.add))
            step(v.tensor_tensor(c(BZ), c(BIH + 1), c(BHH + 1), ALU.add), "cen")
            dve.wait_ge(*PEQ.at("emb"))
            do(v.tensor_copy(w0T[:, :], PS[:, 0, 0:D]))
            do(v.tensor_copy(whT[:, :], PS[:, 1, 0:3 * D]))
            do(v.tensor_copy(flat(raw(R_WIHT, 3)), PS[:, 2, 0:3 * D]))
            do(v.tensor_copy(raw(R_W1T)[:, 0, :], PS[:, 3, 0:D]))
            step(v.tensor_scalar(raw(R_EMBT)[:, 0, 0:TYPES], PS[:, 4, 0:TYPES], c(BM), None, ALU.add), "embc")
            dve.wait_ge(*PEQ.at("wcx"))
            do(v.tensor_copy(wsc[:, :], PS[:, 5, 0:D]))
            do(v.tensor_copy(wnc[:, :], PS[:, 5, D:2 * D]))
            do(v.tensor_copy(flat(wa_b), PS[:, 6, 0:2 * D]))
            do(v.tensor_tensor(bias_r[:, 1, :], PS[0:1, 7, 0:D], row[:, 0, :], ALU.add))
            do(v.tensor_tensor(bias_r[:, 2, :], PS[0:1, 7, D:2 * D], bias_r[:, 1, :], ALU.add))
            do(v.tensor_copy(wcT[:, :], PS[:, 0, 0:3 * D]))
            do(v.tensor_copy(wcE[:, :], PS[0:TYPES, 1, 0:3 * D]))
            for k in range(3):
                do(v.tensor_copy(parts[:, k, :, :], bias_r[:, :, :]))
                do(v.tensor_copy(part_f[:, :, :], parts[:, k, :, :]))
                do(v.tensor_tensor(bias_r[:, :, :], bias_r[:, :, :], part_f[:, :, :], ALU.subtract))
            step(v.memset(ones3[:, :], 1.0), "parts")
            dve.wait_ge(bounce, 64)
            do(v.memset(S[:, :, D], 1.0))
            step(v.memset(flat(BUF[:, :, :]), 0.0), "wcx")

            def bn_stage(q, name, stats, source, *needs):
                def f(g, r):
                    if q.old(g, 1):
                        dve.wait_ge(*q.done(name.replace("bn", "ag"), g - 1))
                    for n in needs:
                        dve.wait_ge(*n(g, r))
                    src_ = source(r)
                    n_ = src_.shape[1]
                    for j in range(n_):
                        ins = v.bn_stats(stats[:, j, :], src_[:, j, :])
                    ins.then_inc(st[name], 1)
                return f

            def ag_stage(q, name, after, stats, mv, n=W):
                def f(g, r):
                    dve.wait_ge(*q.done(after, g))
                    hold()
                    for j in range(n):
                        ins = v.bn_aggr(mv[:, r, j, :], stats[:, j, :])
                    ins.then_inc(st[name], 1)
                return f

            def rc_stage(q, name, after, root, inv):
                def f(g, r):
                    dve.wait_ge(*q.done(after, g))
                    v.reciprocal(inv[:, r, :], root[:, r, :]).then_inc(st[name], 1)
                return f

            def nm_stage(q, name, after, mv, inv, nm):
                def f(g, r):
                    dve.wait_ge(*q.done(after, g))
                    v.scalar_tensor_tensor(nm[:, r, :], mv[:, r, :, 0], -1.0, inv[:, r, :], ALU.mult, ALU.mult)\
                        .then_inc(st[name], 1)
                return f

            def ya_stage(q, source, terms, *needs):
                def f(g, r):
                    for n in needs:
                        dve.wait_ge(*n(g, r))
                    dve.wait_ge(*q.done("y", g))
                    v.tensor_tensor(source(r), source(r), terms(r), ALU.add).then_inc(st["ya"], 1)
                return f

            def ybank(b0):
                return lambda r: wide(b0 + 2 * (r % 2))

            def bc(t, r, n=W):
                return t[:, r, 0:n].unsqueeze(2).to_broadcast([P, n, D])

            def first_layer(name):
                q = ph[name]
                slot = name == "L0"
                o = 1 if slot else 0
                H = lambda r: ring(A3_, r % 2)
                XN = (lambda r: ring(A_, r % 2)) if slot else (lambda r: ring(A_, r))

                def relu(g, r):
                    dve.wait_ge(*q.done("h", g))
                    dve.wait_ge(*q.moved("ldx", g, r))
                    if q.old(g, 2):
                        dve.wait_ge(*q.done("xn", g - 2))
                    v.scalar_tensor_tensor(H(r), wide(6), 0.0, ring(X_, r), ALU.max, ALU.add).then_inc(st["rel"], 1)

                def gamma(g, r):
                    dve.wait_ge(*q.done("xn", g))
                    v.tensor_tensor(XN(r), XN(r), gam_b[:, :].unsqueeze(1).to_broadcast([P, W, D]), ALU.mult)\
                        .then_inc(st["gm"], 1)

                prod = gring[:, 0:2, :, :].rearrange("p a b d -> p (a b) d")

                def sdots(g, r):
                    if q.old(g, 1):
                        dve.wait_ge(*q.done("sdp", g - 1))
                    dve.wait_ge(*q.done("apa", g))
                    v.tensor_tensor(prod, ring(O_, r), wa_b[:, 1, :].unsqueeze(1).to_broadcast([P, W, D]),
                                    ALU.mult).then_inc(st["sdp"], 1)
                    dve.wait_ge(*q.done("sdp", g, 1))
                    hold()
                    v.tensor_reduce(tiles(sD, g, W), prod, AX, ALU.add).then_inc(st["sdp"], 1)

                bn1 = bn_stage(q, "bn1", st1, H if slot else (lambda r: ring(X_, r)),
                               (lambda g, r: q.done("rel", g)) if slot else (lambda g, r: q.moved("ldx", g, r)))
                bn2 = bn_stage(q, "bn2", st2, ybank(0), lambda g, r: q.done("ya", g))
                stages = ([(1, relu)] if slot else []) + [
                    (o, bn1),
                    (1 + o, rc_stage(q, "rc1", "sq1", sd1, rs1)),
                    (3 + o, rc_stage(q, "rc2", "sq2", sd2, rs2)),
                    (3 + o, nm_stage(q, "nm2", "rc2", mv2, rs2, nm2)),
                    (1 + o, nm_stage(q, "nm1", "rc1", mv1, rs1, nm1)),
                    (2 + o, gamma),
                    (o, ag_stage(q, "ag1", "bn1", st1, mv1)),
                    (2 + o, ya_stage(q, ybank(0), XN, lambda g, r: q.done("gm", g))),
                    (2 + o, bn2),
                    (2 + o, ag_stage(q, "ag2", "bn2", st2, mv2))] + ([(4 + o, sdots)] if slot else [])
                pipeline(dve, q.steps, stages)
                finish(dve, name)

            def column(t, g, j):
                return t[:, DS(g * 4 + j, 1)] if not isinstance(g, int) else t[:, g * 4 + j:g * 4 + j + 1]

            def sums(name, weight=None):
                q = ph[name]
                pairs = name != "S0"

                def match(g, r):
                    dve.wait_ge(*q.moved("ldg", g, r))
                    if q.old(g):
                        dve.wait_ge(*q.done("sm", g - R))
                    def one(o, tile, like, by=None):
                        ids = ring(DB_, r, 4)[:, tile, :]
                        if by is None:
                            return v.tensor_scalar(o, ids, like, None, ALU.is_equal)
                        return v.tensor_scalar(o, ids, like, by, ALU.is_equal, ALU.mult)

                    for j in range(4):
                        w_ = None if weight is None else column(weight, g, j)
                        ins = one(ring(MM_, r, 4)[:, j, :], j, column(dstc, g, j), w_)
                        if not pairs:
                            ins = one(ring(MC_, r, 4)[:, j, :], j, column(dprev, g, j))
                        elif j % 2 == 0:
                            one(ring(MX_, r, 2)[:, j // 2, :], j + 1, column(dstc, g, j), w_)
                            ins = one(ring(MC_, r, 4)[:, j:j + 2, :], slice(j, j + 2), column(dprev, g, j))
                    ins.then_inc(st["mk"], 1)

                def scale(g, r):
                    dve.wait_ge(*q.done("cv", g))
                    if name == "S0":
                        hold()
                        v.reciprocal(tiles(rdeg, g, 4), osum(r)[:, :, D + TYPES]).then_inc(st["qq"], 1)
                        return
                    if name == "S1":
                        v.tensor_scalar(nm1[:, r, 0:4], osum(r)[:, :, D], 1e-6, None, ALU.max).then_inc(st["qq"], 1)
                        dve.wait_ge(*q.done("qq", g, 1))
                        v.reciprocal(rs1[:, r, 0:4], nm1[:, r, 0:4]).then_inc(st["qq"], 1)
                        dve.wait_ge(*q.done("qq", g, 2))
                        by = bc(rs1, r, 4)
                    else:
                        by = tiles(rdeg, g, 4).unsqueeze(2).to_broadcast([P, 4, D])
                    if q.old(g):
                        dve.wait_ge(*q.moved("sto", g - R, r))
                    v.tensor_tensor(ring(QB_, r, 4), osum(r)[:, :, 0:D], by, ALU.mult).then_inc(st["qq"], 1)
                pipeline(dve, q.steps, [(0, match)] + ([(2, scale)] if name != "S3" else []))
                finish(dve, name)

            first_layer("A")
            finish(dve, "G0")
            for k in range(TYPES):
                do(v.tensor_scalar(oh[:, :, k], typec[:, :], float(k), None, ALU.is_equal))
            step(v.memset(oh[:, :, TYPES], 1.0), "oh")
            sums("S0")
            finish(dve, "GD")
            first_layer("L0")

            q = ph["B"]

            def q0(g, r):
                dve.wait_ge(*q.done("rc1", g))
                v.tensor_tensor(rs3[:, r, :], rs1[:, r, :], rs1[:, r, :], ALU.mult).then_inc(st["q"], 1)

            def q1(g, r):
                dve.wait_ge(*q.done("q", g, 1))
                v.tensor_tensor(rs3[:, r, :], rs3[:, r, :], mv1[:, r, :, 1], ALU.mult).then_inc(st["q"], 1)

            def u(g, r):
                dve.wait_ge(*q.done("r3", g))
                dve.wait_ge(*q.done("xn", g))
                if q.old(g, 2):
                    dve.wait_ge(*q.done("tr", g - 2))
                v.tensor_tensor(ring(A3_, r % 2), ring(A_, r), bc(rs3, r), ALU.mult).then_inc(st["u"], 1)
            pipeline(dve, q.steps, [
                (0, bn_stage(q, "bn1", st1, lambda r: ring(X_, r), lambda g, r: q.moved("ldx", g, r))),
                (5, rc_stage(q, "rc2", "sq2", sd2, rs2)),
                (1, rc_stage(q, "rc1", "sq1", sd1, rs1)),
                (2, rc_stage(q, "r3", "sq3", sd3, rs3)),
                (5, nm_stage(q, "nm2", "rc2", mv2, rs2, nm2)),
                (1, nm_stage(q, "nm1", "rc1", mv1, rs1, nm1)),
                (1, q0),
                (2, u),
                (1, q1),
                (4, ya_stage(q, ybank(2), lambda r: ring(A_, r))),
                (0, ag_stage(q, "ag1", "bn1", st1, mv1)),
                (4, bn_stage(q, "bn2", st2, ybank(2), lambda g, r: q.done("ya", g))),
                (4, ag_stage(q, "ag2", "bn2", st2, mv2))])
            finish(dve, "B")

            finish(dve, "G1")
            ssq = sem("ssq")

            dsum = sem("dsum")

            def prods(g, r):
                if q.old(g, 2):
                    dve.wait_ge(dsum, g - 1)
                v.tensor_tensor(ring(X_, r % 2), tiles(S, g, W)[:, :, 0:D], wa_b[:, 0, :].unsqueeze(1).to_broadcast([P, W, D]),
                                ALU.mult).then_inc(ssq, 1)

            def dots(g, r):
                dve.wait_ge(ssq, g + 1)
                hold()
                v.tensor_reduce(tiles(sS, g, W), ring(X_, r % 2), AX, ALU.add).then_inc(dsum, 1)
            pipeline(dve, T // W, [(0, prods), (1, dots)])
            dve.wait_ge(dsum, T // W)
            hold()
            do(v.tensor_tensor(sD[:, :], sD[:, :], lastc[:, :], ALU.mult))
            do(v.tensor_scalar(mx[:, :], lastc[:, :], -1.0, NEG, ALU.add, ALU.mult))
            step(v.tensor_tensor(sD[:, :], sD[:, :], mx[:, :], ALU.add), "sDv")
            dve.wait_ge(SPQ, 5)
            do(v.tensor_tensor(penF[:, 1:T], dP[:, 1:T], dP[:, 0:T - 1], ALU.is_equal))
            do(v.tensor_scalar(penF[:, 1:T], penF[:, 1:T], -1.0, NEG, ALU.add, ALU.mult))
            do(v.memset(penF[:, 0:1], -NEG))
            do(v.tensor_copy(penB[:, 0:T - 1], penF[:, 1:T]))
            do(v.memset(penB[:, T - 1:T], -NEG))
            rw = lambda k: row[:, k, :]
            do(v.memset(rw(6), -NEG))
            do(v.tensor_tensor(row[:, 6, 1:P], row[:, 4, 1:P], row[:, 5, 0:P - 1], ALU.is_equal))
            do(v.tensor_scalar(row[:, 6, 1:P], row[:, 6, 1:P], -1.0, NEG, ALU.add, ALU.mult))
            do(v.tensor_tensor(rw(7), rw(4), rw(5), ALU.is_equal))
            do(v.tensor_scalar(rw(7), rw(7), -1.0, NEG, ALU.add, ALU.mult))
            do(v.tensor_tensor(rw(4), rw(7), rw(6), ALU.add))
            do(v.memset(rw(5), -NEG))
            do(v.tensor_tensor(row[:, 5, 0:P - 1], row[:, 7, 0:P - 1], row[:, 6, 1:P], ALU.add))
            do(v.memset(rw(3), -NEG))

            def scan(dst_, pen, val, back):
                if back:
                    return v.tensor_tensor_scan(dst_[:, ::-1], pen[:, ::-1], val[:, ::-1], -NEG, ALU.add, ALU.max)
                return v.tensor_tensor_scan(dst_, pen, val, -NEG, ALU.add, ALU.max)

            def spread(tag, back, first):
                pen = penB if back else penF
                step(scan(vb, pen, va, back), tag + "0", SEQ)
                dve.wait_ge(SPQ, first + 2)
                do(scan(rw(2), rw(5) if back else rw(4), rw(1), back))
                if back:
                    do(v.memset(row[:, 3, P - 1:P], -NEG))
                    step(v.tensor_tensor(row[:, 3, 0:P - 1], row[:, 2, 1:P], row[:, 6, 1:P], ALU.add), tag + "2", SEQ)
                else:
                    do(v.memset(row[:, 3, 0:1], -NEG))
                    step(v.tensor_tensor(row[:, 3, 1:P], row[:, 2, 0:P - 1], row[:, 6, 1:P], ALU.add), tag + "2", SEQ)
                dve.wait_ge(SPQ, first + 4)
                at = slice(T - 1, T) if back else slice(0, 1)
                do(v.tensor_tensor(va[:, at], va[:, at], c(CC), ALU.max))
                return scan(vc, pen, va, back)

            dve.wait_ge(*PEQ.at("sdv"))
            step(v.tensor_copy(flat(sq_rows[0]), PS[0:HT, 0, 0:2 * D]), "seqv")
            dve.wait_ge(SPQ, 7)
            step(spread("a", True, 7), "a5", SEQ)
            dve.wait_ge(*PEQ.at("sdb"))
            do(v.tensor_tensor(sS[:, :], sS[:, :], PS[:, 1, 0:T], ALU.add))
            step(v.scalar_tensor_tensor(sS[:, :], sS[:, :], SLOPE, sS[:, :], ALU.mult, ALU.max), "e")
            dve.wait_ge(*PEQ.at("ev"))
            step(v.tensor_copy(flat(sq_rows[0]), PS[0:HT, 2, 0:2 * D]), "seqe")
            dve.wait_ge(SPQ, 15)
            do(spread("b", False, 15))
            do(v.tensor_copy(va, vc))
            step(spread("c", True, 19), "c5", SEQ)
            dve.wait_ge(*PEQ.at("mb"))
            step(v.tensor_tensor(ew[:, :], sS[:, :], PS[:, 3, 0:T], ALU.subtract), "exa")
            dve.wait_ge(*ACQ.at("exp"))
            sums("S1", ew)

            q = ph["L1"]
            pipeline(dve, q.steps, [
                (2, rc_stage(q, "rc2", "sq2", sd2, rs2)),
                (2, nm_stage(q, "nm2", "rc2", mv2, rs2, nm2)),
                (1, ya_stage(q, ybank(2), lambda r: ring(X_, r), lambda g, r: q.moved("ldx", g, r))),
                (1, bn_stage(q, "bn2", st2, ybank(2), lambda g, r: q.done("ya", g))),
                (1, ag_stage(q, "ag2", "bn2", st2, mv2))])
            finish(dve, "L1")

            def newton(q, k, g, r, n):
                if k:
                    dve.wait_ge(*q.done("nw", g, k))
                else:
                    dve.wait_ge(*q.done("ag2", g))
                vv, tt, yy = nwt[:, 0, 0:n], nwt[:, 1, 0:n], rs2[:, r, 0:n]
                if k == 0:
                    ins = v.tensor_scalar(vv, mv2[:, r, 0:n, 1], EPS, None, ALU.add)
                elif k == 1:
                    ins = v.tensor_scalar(nwi[:, 0:n], vv.bitcast(I32), 1, None, ALU.logical_shift_right)
                elif k == 2:
                    ins = v.tensor_scalar(yy.bitcast(I32), nwi[:, 0:n], -1.0, MAGIC, ALU.mult, ALU.add)
                elif k == 12:
                    ins = v.scalar_tensor_tensor(nm2[:, r, 0:n], mv2[:, r, 0:n, 0], -1.0, yy, ALU.mult, ALU.mult)
                elif k % 3 == 0:
                    ins = v.tensor_tensor(tt, yy, yy, ALU.mult)
                elif k % 3 == 1:
                    ins = v.scalar_tensor_tensor(tt, tt, -0.5, vv, ALU.mult, ALU.mult)
                else:
                    ins = v.scalar_tensor_tensor(yy, tt, 1.5, yy, ALU.add, ALU.mult)
                ins.then_inc(st["nw"], 1)

            def gated(name):
                q = ph[name]
                slot = name == "L3"
                n = 4 if slot else W
                halves = 1 if slot else 2
                XT, RN, Z, Y = gated_rings(slot)

                def y(g, r):
                    dve.wait_ge(*q.done("ot", g))
                    if q.old(g, 2):
                        dve.wait_ge(*q.done("apa", g - 2))
                    source = PS[:, 3, :].rearrange("p (t d) -> p t d", d=D) if slot else wide(0)
                    v.tensor_tensor(Y(r), source, ring(X_, r, n), ALU.add).then_inc(st["y"], 1)

                def w(k):
                    def f(g, r):
                        dve.wait_ge(*(q.done("w", g, k) if k else q.done("th", g)))
                        if k == 0:
                            ins = v.tensor_tensor(XT(r), XT(r), RN(r), ALU.subtract)
                        elif k == 1:
                            ins = v.tensor_tensor(XT(r), XT(r), Z(r), ALU.mult)
                        else:
                            ins = v.tensor_tensor(XT(r), XT(r), RN(r), ALU.add)
                        ins.then_inc(st["w"], 1)
                    return f

                def tn(h):
                    def f(g, r):
                        dve.wait_ge(*q.done(f"sg{h}", g))
                        a = flat(RN(r))[:, 512 * h:512 * (h + 1)]
                        v.scalar_tensor_tensor(a, PS[:, 6 if slot else 4 + 3 * h, :], c(BHH + 2), a, ALU.add, ALU.mult)\
                            .then_inc(st["tn"], 1)
                    return f

                def tn_in(g, r):
                    dve.wait_ge(*q.done("tn", g, 1))
                    v.tensor_tensor(flat(RN(r)), flat(RN(r)), PS[:, 7, :], ALU.add).then_inc(st["tn"], 1)

                def nw(*ks):
                    def f(g, r):
                        for k in ks:
                            if q.old(g) and k == 2:
                                dve.wait_ge(*q.done("apa", g - R))
                            newton(q, k, g, r, n)
                    return f
                bn = bn_stage(q, "bn2", st2, Y, lambda g, r: q.done("y", g))
                pipeline(dve, q.steps, [
                    (4, nw(0)), (2, w(0)), (4, nw(1)), (2, w(1)), (4, nw(2)), (2, w(2)), (4, nw(3)), (3, y),
                    (1, tn(0)), (4, nw(4)), (1, tn_in if slot else tn(1)), (4, nw(5)),
                    (3, bn), (4, nw(6, 7, 8, 9, 10, 11, 12)), (3, ag_stage(q, "ag2", "bn2", st2, mv2, n))])
                finish(dve, name)

            gated("C1")

            finish(dve, "G2")
            vsq = sem("vsq")

            def row_var(g, r):
                if q.old(g, 1):
                    dve.wait_ge(vsq, g * 3)
                    hold()
                for j in range(W):
                    one = S[:, DS(g * W + j, 1), 0:D] if not isinstance(g, int) else S[:, g * W + j:g * W + j + 1, 0:D]
                    ins = v.bn_stats(st1[:, j, :], one.rearrange("p o d -> p (o d)"))
                ins.then_inc(vsq, 1)
                dve.wait_ge(vsq, g * 3 + 1)
                hold()
                for j in range(W):
                    ins = v.bn_aggr(mv1[:, 0, j, :], st1[:, j, :])
                ins.then_inc(vsq, 1)
                dve.wait_ge(vsq, g * 3 + 2)
                hold()
                v.tensor_scalar(tiles(mx, g, W), mv1[:, 0, :, 1], EPS, None, ALU.add).then_inc(vsq, 1)
            pipeline(dve, T // W, [(0, row_var)])
            dve.wait_ge(vsq, 3 * (T // W))
            hold()
            do(v.reciprocal(mx[:, :], mx[:, :]))
            step(v.tensor_copy(sD[:, :], mx[:, :]), "rv")
            dve.wait_ge(*ACQ.at("rv"))
            sums("S2", ew)

            q = ph["L2"]
            pipeline(dve, q.steps, [
                (0, bn_stage(q, "bn1", st1, lambda r: ring(X_, r), lambda g, r: q.moved("ldx", g, r))),
                (1, rc_stage(q, "rc1", "sq1", sd1, rs1)),
                (4, rc_stage(q, "rc2", "sq2", sd2, rs2)),
                (1, nm_stage(q, "nm1", "rc1", mv1, rs1, nm1)),
                (4, nm_stage(q, "nm2", "rc2", mv2, rs2, nm2)),
                (3, ya_stage(q, ybank(2), lambda r: ring(X_, r))),
                (0, ag_stage(q, "ag1", "bn1", st1, mv1)),
                (3, bn_stage(q, "bn2", st2, ybank(2), lambda g, r: q.done("ya", g))),
                (3, ag_stage(q, "ag2", "bn2", st2, mv2))])
            finish(dve, "L2")
            gated("C2")
            finish(dve, "G3")
            sums("S3")
            gated("L3")

        @block.tensor
        def _(pe):
            te = nc.tensor
            pe.wait_ge(*POOL.at("ident"))
            pe.wait_ge(*V.at("idf"))
            for k in (0, 2, 3, 4, 5):
                for h in range(2):
                    ins = te.transpose(PS[:, k, h * HT:(h + 1) * HT], RF[0:HT, k, h, :], ident[0:HT, 0:HT])
            PEQ.did(ins, "ids")
            pe.wait_ge(*V.at("idx"))
            pe.wait_ge(*V.at("cen"))
            te.transpose(PS[:, 0, 0:D], raw(R_W0)[:, 0, :], ident[:, :])
            for k in range(3):
                te.transpose(PS[:, 1, k * D:(k + 1) * D], raw(R_WHH + k)[:, 0, :], ident[:, :])
                te.transpose(PS[:, 2, k * D:(k + 1) * D], raw(R_WIH + k)[:, 0, :], ident[:, :])
            te.transpose(PS[:, 3, 0:D], raw(R_W1)[:, 0, :], ident[:, :])
            PEQ.did(te.transpose(PS[:, 4, 0:TYPES], raw(R_EMB)[0:TYPES, 0, :], ident[0:TYPES, 0:TYPES]), "emb")

            def mm(o, a, b, start=True, stop=True):
                return te.matmul(o, a, b, start=start, stop=stop)
            mm(PS[:, 5, 0:D], cen[:, :], raw(R_GWS)[:, 0, :])
            mm(PS[:, 5, D:2 * D], cen[:, :], raw(R_GWN)[:, 0, :])
            pe.wait_ge(*V.at("embc"))
            for k in range(2):
                mm(PS[:, 6, k * D:(k + 1) * D], raw(R_AA + k)[:, 0, :], raw(R_W1T)[:, 0, :])
            mm(PS[0:1, 7, 0:D], c(B2), raw(R_WS)[:, 0, :])
            mm(PS[0:1, 7, D:2 * D], c(B2), raw(R_WN)[:, 0, :])
            mm(PS[:, 0, 0:3 * D], raw(R_WM)[:, 0, :], flat(raw(R_WIHT, 3)))
            PEQ.did(mm(PS[0:TYPES, 1, 0:3 * D], raw(R_EMBT)[:, 0, 0:TYPES], flat(raw(R_WIHT, 3))), "wcx")
            pe.wait_ge(*V.at("wcx"))
            pe.wait_ge(bounce, 64)

            def turn(o, source, n):
                for j in range(n):
                    ins = te.transpose(o[:, j, :], source[:, j, :], ident[:, :])
                return ins

            def total(b, terms, bias):
                for h in range(2):
                    if bias is not None:
                        mm(wide(b)[:, 4 * h:4 * h + 4, :], ones3[:, :], bias3[:, bias:bias + 1, :].to_broadcast([3, 4, D]),
                           True, False)
                    for j in range(4 * h, 4 * h + 4):
                        for k, (left, right) in enumerate(terms):
                            ins = mm(wide(b)[:, j, :], left[:, j, :], right[:, :], bias is None and k == 0,
                                     k == len(terms) - 1 and (bias is None or j == 4 * h + 3))
                return ins

            def first_layer(name):
                q = ph[name]
                slot = name == "L0"
                o = 1 if slot else 0
                base_rows = lambda r: ring(X_, r)

                def tr(g, r):
                    pe.wait_ge(*q.moved("ldg", g, r))
                    if q.old(g, 1):
                        pe.wait_ge(*q.done("ev", g - 1))
                    turn(wide(4), ring(G_, r), W).then_inc(st["tr"], 1)

                def h(g, r):
                    pe.wait_ge(*q.done("ev", g))
                    if q.old(g, 1):
                        pe.wait_ge(*q.done("rel", g - 1))
                    for j in range(W):
                        ins = mm(wide(6)[:, j, :], ring(A2_, r % 2)[:, j, :], w0T[:, :])
                    ins.then_inc(st["h"], 1)

                def y(g, r):
                    pe.wait_ge(*q.moved("ldx", g, r))
                    if q.old(g, 2):
                        pe.wait_ge(*q.done("apa", g - 2))
                    b = 2 * (r % 2)
                    for hh in range(2):
                        yo = wide(b)[:, 4 * hh:4 * hh + 4, :]
                        mm(yo, ident[:, :], base_rows(r)[:, 4 * hh:4 * hh + 4, :], True, False)
                        ins = mm(yo, ones3[:, :], bias3[:, 0:1, :].to_broadcast([3, 4, D]), False, True)
                    ins.then_inc(st["y"], 1)
                pipeline(pe, q.steps, ([(0, tr), (1, h)] if slot else []) + [(1 + o, y)])
                finish(pe, name)

            def sums(name, more=None, width=D):
                q = ph[name]

                def product(g, r, j):
                    k = g * 4 + j
                    t_ = (lambda a: a[:, DS(k, 1)]) if not isinstance(g, int) else (lambda a: a[:, k:k + 1])
                    m = ring(MM_, r, 4)[:, j, :]
                    n = width if more is None else D
                    mm(PS[:, j, 0:n], m, t_(S)[:, :, 0:n].rearrange("p o d -> p (o d)"), True, False)
                    if more is not None:
                        mm(PS[:, j, D:width], m, more(t_), False, False)

                def carry(g, r, j):
                    if j or not isinstance(g, int) or g:
                        pe.wait_ge(*q.done("cv", g, j))
                    last_ = osum(r)[:, j - 1, 0:width] if j else osum((r - 1) % R)[:, 3, 0:width]
                    mm(PS[:, j, 0:width], ring(MC_, r, 4)[:, j, :], last_, False, True).then_inc(st["sm"], 1)

                def one(g, r):
                    pe.wait_ge(*q.done("mk", g))
                    if q.old(g, 1):
                        pe.wait_ge(*q.done("cv", g - 1, 3))
                    product(g, r, 0)
                    product(g, r, 1)
                    for j in range(4):
                        carry(g, r, j)
                        if j < 2:
                            product(g, r, j + 2)
                def products(k):
                    def f(g, r):
                        if k == 0:
                            pe.wait_ge(*q.done("mk", g))
                        if q.old(g, 2):
                            pe.wait_ge(*q.done("cv", g - 2))
                        for j, of, m in ((2 * k, 2 * k, ring(MM_, r, 4)[:, 2 * k, :]),
                                         (2 * k + 1, 2 * k + 1, ring(MM_, r, 4)[:, 2 * k + 1, :]),
                                         (2 * k + 1, 2 * k, ring(MX_, r, 2)[:, k, :])):
                            n = g * 4 + of
                            rows_ = S[:, DS(n, 1), 0:width] if not isinstance(g, int) else S[:, n:n + 1, 0:width]
                            mm(PS[:, bank_of(r, j), 0:width], m, rows_.rearrange("p o d -> p (o d)"), of == j, False)
                    return f

                def carries(k):
                    def f(g, r):
                        if k:
                            pe.wait_ge(*q.done("cv", g, 1))
                            last_ = osum(r)[:, 1, 0:width]
                        else:
                            if q.old(g, 1):
                                pe.wait_ge(*q.done("cv", g - 1, 3))
                            last_ = osum((r - 1) % R)[:, 3, 0:width]
                        for j in (2 * k + 1, 2 * k):
                            mm(PS[:, bank_of(r, j), 0:width], ring(MC_, r, 4)[:, j, :], last_, False, True)\
                                .then_inc(st["sm"], 1)
                    return f

                if name == "S0":
                    pipeline(pe, q.steps, [(0, one)])
                else:
                    pipeline(pe, q.steps, [(0, products(0)), (1, carries(1)), (0, products(1)), (0, carries(0))])
                finish(pe, name)

            first_layer("A")
            finish(pe, "G0")
            pe.wait_ge(*V.at("oh"))
            sums("S0", lambda t_: t_(oh).rearrange("p o d -> p (o d)"), D + CNT)
            first_layer("L0")

            q = ph["B"]

            def trB(g, r):
                pe.wait_ge(*q.done("u", g))
                if q.old(g, 1):
                    pe.wait_ge(*q.done("ev", g - 1))
                turn(wide(0), ring(A3_, r % 2), W).then_inc(st["tr"], 1)

            def yB(g, r):
                pe.wait_ge(*q.done("ev", g))
                if q.old(g, 2):
                    pe.wait_ge(*q.done("apa", g - 2))
                total(2 + 2 * (r % 2), [(ring(A4_, r % 2), wsc)], 1).then_inc(st["y"], 1)
            pipeline(pe, q.steps, [(3, yB), (2, trB)])
            finish(pe, "B")

            pe.wait_ge(*V.at("sDv"))

            def to_rows(o, source, name):
                for h in range(2):
                    ins = te.transpose(o[:, h * D:(h + 1) * D], source[:, h * HT:(h + 1) * HT], ident[:, :])
                PEQ.did(ins, name)

            def to_cols(o, name):
                for h in range(2):
                    ins = te.transpose(o[:, h * HT:(h + 1) * HT], sq_rows[1][:, h, :], ident[0:HT, 0:HT])
                PEQ.did(ins, name)
            to_rows(PS[0:HT, 0, :], sD, "sdv")
            pe.wait_ge(SPQ, 13)
            to_cols(PS[:, 1, :], "sdb")
            pe.wait_ge(*V.at("e"))
            to_rows(PS[0:HT, 2, :], sS, "ev")
            pe.wait_ge(SPQ, 25)
            to_cols(PS[:, 3, :], "mb")
            pe.wait_ge(*V.at("exa"))
            pe.wait_ge(*ACQ.at("exp"))
            sums("S1", None, D + 1)

            q = ph["L1"]

            def trG(g, r):
                pe.wait_ge(*q.moved("ldg", g, r))
                if q.old(g, 1):
                    pe.wait_ge(*q.done("ev", g - 1))
                turn(wide(0), ring(G_, r), W).then_inc(st["tr"], 1)

            def y1(g, r):
                pe.wait_ge(*q.done("ev", g))
                if q.old(g, 2):
                    pe.wait_ge(*q.done("apa", g - 2))
                total(2 + 2 * (r % 2), [(ring(A2_, r % 2), w1s)], None).then_inc(st["y"], 1)
            pipeline(pe, q.steps, [(0, trG), (0, y1)])
            finish(pe, "L1")

            def gated(name):
                q = ph[name]
                slot = name == "L3"
                n = 4 if slot else W
                XT, RN, Z, Y = gated_rings(slot)

                def ot(g, r):
                    pe.wait_ge(*q.done("w", g))
                    if q.old(g, 1):
                        pe.wait_ge(*q.done("y", g - 1))
                    if slot:
                        turn(PS[:, 3, :].rearrange("p (t d) -> p t d", d=D), XT(r), n).then_inc(st["ot"], 1)
                        return
                    if isinstance(g, int):
                        pe.wait_ge(*q.done("ev", min(g + 2, q.steps - 1)))
                    else:
                        pe.wait_ge(*q.done("ev", g + 2))
                    turn(wide(0), XT(r), n).then_inc(st["ot"], 1)

                def tr(g, r):
                    pe.wait_ge(*q.moved("ldx", g, r))
                    if q.old(g, 3):
                        pe.wait_ge(*q.done("y", g - 3))
                    if q.old(g, 1):
                        pe.wait_ge(*q.done("ev", g - 1))
                    turn(wide(0), ring(X_, r), n).then_inc(st["tr"], 1)

                def gates(h):
                    def f(g, r):
                        pe.wait_ge(*q.done("ev", g))
                        if q.old(g, 1):
                            pe.wait_ge(*q.done(f"sg{h}", g - 1))
                            pe.wait_ge(*q.done("tn", g - 1, h + 1))
                        for k in range(3):
                            ins = mm(PS[:, 2 + 3 * h + k, :], whT[:, k * D:(k + 1) * D],
                                     flat(XT(r))[:, 512 * h:512 * (h + 1)])
                        ins.then_inc(st[f"g{h}"], 1)
                    return f

                def slot_turns(g, r):
                    pe.wait_ge(*q.moved("ldx", g, r))
                    pe.wait_ge(*q.moved("ldg", g, r))
                    pe.wait_ge(*q.moved("ldc", g, r))
                    if q.old(g, 1):
                        pe.wait_ge(*q.done("ev", g - 1))
                    turn(PS[:, 0, :].rearrange("p (t d) -> p t d", d=D), ring(X_, r, 4), 4).then_inc(st["tr"], 1)
                    if q.old(g, 1):
                        pe.wait_ge(*q.done("eg", g - 1))
                    turn(PS[:, 1, :].rearrange("p (t d) -> p t d", d=D), ring(G_, r, 4), 4).then_inc(st["tg"], 1)
                    if q.old(g, 1):
                        pe.wait_ge(*q.done("ec", g - 1))
                    turn(PS[0:CNT, 2, :].rearrange("p (t d) -> p t d", d=D), cring(r), 4).then_inc(st["tc"], 1)

                def slot_gates(g, r):
                    for k in ("ev", "eg", "ec"):
                        pe.wait_ge(*q.done(k, g))
                    if q.old(g, 1):
                        pe.wait_ge(*q.done("sg0", g - 1))
                        pe.wait_ge(*q.done("tn", g - 1))
                    gt, ct = flat(ring(64, r % 2, 4)), flat(ring(20, r % 2, 4))[0:TYPES]
                    for k in range(3):
                        a = slice(k * D, (k + 1) * D)
                        mm(PS[:, 4 + k, :], whT[:, a], flat(XT(r)), True, k == 2)
                        b = 4 + k if k < 2 else 7
                        mm(PS[:, b, :], wcT[:, a], gt, k == 2, False)
                        ins = mm(PS[:, b, :], wcE[:, a], ct, False, True)
                    ins.then_inc(st["g0"], 1)
                if slot:
                    pipeline(pe, q.steps, [(3, ot), (0, slot_turns), (1, slot_gates)])
                else:
                    pipeline(pe, q.steps, [(3, ot), (1, gates(0)), (1, gates(1)), (0, tr)])
                finish(pe, name)

            gated("C1")
            finish(pe, "G2")
            sums("S2")

            q = ph["L2"]

            def turns(g, r):
                pe.wait_ge(*q.done("u", g))
                if q.old(g, 1):
                    pe.wait_ge(*q.done("ev", g - 1))
                turn(wide(0), ring(A_, r % 2), W).then_inc(st["tr"], 1)
                pe.wait_ge(*q.moved("ldg", g, r))
                if q.old(g, 1):
                    pe.wait_ge(*q.done("eg", g - 1))
                turn(wide(6), ring(G_, r), W).then_inc(st["tg"], 1)

            def y2(g, r):
                pe.wait_ge(*q.done("ev", g))
                pe.wait_ge(*q.done("eg", g))
                if q.old(g, 2):
                    pe.wait_ge(*q.done("apa", g - 2))
                total(2 + 2 * (r % 2), [(ring(A2_, r % 2), wsc), (ring(A3_, r % 2), wnc)], 2)\
                    .then_inc(st["y"], 1)
            pipeline(pe, q.steps, [(1, turns), (2, y2)])
            finish(pe, "L2")
            gated("C2")
            finish(pe, "G3")
            sums("S3")
            gated("L3")

        @block.scalar
        def _(act):
            s = nc.scalar
            act.wait_ge(*V.at("wcx"))

            def root(q, name, after, out_, source):
                def f(g, r):
                    act.wait_ge(*q.done(after, g))
                    s.activation(out_[:, r, :], source(r), ACT.Sqrt, bias=epsc[:, :]).then_inc(st[name], 1)
                return f

            def apply_stage(q, source, first=0, n=W, stored=True, scatters=False, extra=(), after="nm2"):
                def f(g, r):
                    act.wait_ge(*q.done(after, g))
                    if q.old(g):
                        if stored:
                            act.wait_ge(*q.moved("sto", g - R, r))
                        if scatters:
                            act.wait_ge(*q.moved("sct", g - R, r))
                        for k in extra:
                            act.wait_ge(*q.done(k, g - R))
                    for j in range(first, n):
                        ins = s.activation(ring(O_, r, n)[:, j, :], source(r)[:, j, :], ACT.Identity,
                                           bias=nm2[:, r, j:j + 1], scale=rs2[:, r, j:j + 1])
                    ins.then_inc(st["apa"], 1)
                return f

            def ybank(b0):
                return lambda r: wide(b0 + 2 * (r % 2))

            def copy(q, name, after, dest, source, reuse, n):
                def f(g, r):
                    act.wait_ge(*q.done(after, g))
                    if q.old(g, n):
                        act.wait_ge(*q.done(reuse, g - n))
                    s.activation(dest(r), source, ACT.Copy).then_inc(st[name], 1)
                return f

            def var(t):
                return lambda r: t[:, r, :, 1]

            def rows_by(dest, source, g, r, name):
                for j in range(W):
                    ins = s.activation(dest[:, j, :], source[:, j, :], ACT.Identity, bias=nm1[:, r, j:j + 1],
                                       scale=rs1[:, r, j:j + 1])
                ins.then_inc(st[name], 1)

            def first_layer(name):
                q = ph[name]
                slot = name == "L0"
                o = 1 if slot else 0
                rows_ = (lambda r: ring(A3_, r % 2)) if slot else (lambda r: ring(X_, r))

                def xn(g, r):
                    act.wait_ge(*q.done("nm1", g))
                    if q.old(g, 2 if slot else R):
                        act.wait_ge(*q.done("ya", g - (2 if slot else R)))
                    rows_by(ring(A_, r % 2) if slot else ring(A_, r), rows_(r), g, r, "xn")
                stages = [(3 + o, apply_stage(q, ybank(0), scatters=slot, extra=("sdp",) if slot else ())), (1 + o, xn),
                          (o, root(q, "sq1", "ag1", sd1, var(mv1))), (2 + o, root(q, "sq2", "ag2", sd2, var(mv2)))]
                if slot:
                    stages = [(0, copy(q, "ev", "tr", lambda r: ring(A2_, r % 2), wide(4), "h", 2))] + stages
                pipeline(act, q.steps, stages)
                finish(act, name)

            def sums(name, width=D):
                q = ph[name]

                def one(g, r):
                    if q.old(g):
                        if "sto" in q.dmas:
                            act.wait_ge(*q.moved("sto", g - R, r))
                        if "qq" in q.mult:
                            act.wait_ge(*q.done("qq", g - R))
                    pairs = name != "S0"
                    for k, j in enumerate((1, 0, 3, 2) if pairs else range(4)):
                        act.wait_ge(*q.done("sm", g, k + 1))
                        s.activation(osum(r)[:, j, 0:width], PS[:, bank_of(r, j) if pairs else j, 0:width], ACT.Copy)\
                            .then_inc(st["cv"], 1)
                pipeline(act, q.steps, [(0, one)])
                finish(act, name)

            first_layer("A")
            sums("S0", D + CNT)
            first_layer("L0")

            q = ph["B"]

            def x2(g, r):
                act.wait_ge(*q.done("nm1", g))
                if q.old(g):
                    act.wait_ge(*q.moved("st2", g - R, r))
                    act.wait_ge(*q.done("ya", g - R))
                rows_by(ring(A_, r), ring(X_, r), g, r, "xn")
            pipeline(act, q.steps, [
                (5, apply_stage(q, ybank(2))),
                (3, copy(q, "ev", "tr", lambda r: ring(A4_, r % 2), wide(0), "y", 2)),
                (1, x2),
                (1, root(q, "sq3", "q", sd3, lambda r: rs3[:, r, :])),
                (0, root(q, "sq1", "ag1", sd1, var(mv1))),
                (4, root(q, "sq2", "ag2", sd2, var(mv2)))])
            finish(act, "B")
            act.wait_ge(*V.at("exa"))
            ACQ.did(s.activation(ew[:, :], ew[:, :], ACT.Exp), "exp")
            act.wait_ge(*ACQ.at("exp"))
            sums("S1", D + 1)
            q = ph["L1"]
            pipeline(act, q.steps, [
                (2, apply_stage(q, ybank(2), scatters=True)),
                (0, copy(q, "ev", "tr", lambda r: ring(A2_, r % 2), wide(0), "y", 2)),
                (1, root(q, "sq2", "ag2", sd2, var(mv2)))])
            finish(act, "L1")

            def gated(name):
                q = ph[name]
                slot = name == "L3"
                n = 4 if slot else W
                XT, RN, Z, Y = gated_rings(slot)

                def th(g, r):
                    act.wait_ge(*q.done("tn", g))
                    s.activation(flat(RN(r)), flat(RN(r)), ACT.Tanh, bias=c(BIH + 2)).then_inc(st["th"], 1)

                def sg(h):
                    def f(g, r):
                        act.wait_ge(*q.done(f"g{h}", g))
                        if q.old(g, 2):
                            act.wait_ge(*q.done("w", g - 2))
                        b = 4 if slot else 2 + 3 * h
                        a = slice(512 * h, 512 * (h + 1))
                        s.activation(flat(RN(r))[:, a], PS[:, b, :], ACT.Sigmoid, bias=c(BR))
                        s.activation(flat(Z(r))[:, a], PS[:, b + 1, :], ACT.Sigmoid, bias=c(BZ)).then_inc(st[f"sg{h}"], 1)
                    return f
                last_ = apply_stage(q, Y, 0, n, stored=not slot, scatters=slot, after="nw")
                if slot:
                    pipeline(act, q.steps, [
                        (2, th), (5, last_),
                        (0, copy(q, "ev", "tr", lambda r: flat(XT(r)), PS[:, 0, :], "ot", R)),
                        (0, copy(q, "eg", "tg", lambda r: flat(ring(64, r % 2, 4)), PS[:, 1, :], "g0", 2)),
                        (0, copy(q, "ec", "tc", lambda r: flat(ring(20, r % 2, 4))[0:CNT], PS[0:CNT, 2, :], "g0", 2)),
                        (1, sg(0))])
                else:
                    pipeline(act, q.steps, [
                        (2, th), (5, last_), (1, sg(0)), (1, sg(1)),
                        (0, copy(q, "ev", "tr", lambda r: XT(r), wide(0), "ot", R))])
                finish(act, name)

            gated("C1")
            act.wait_ge(*V.at("rv"))
            ACQ.did(s.activation(ew[:, :], sD[:, :], ACT.Sqrt), "rv")
            sums("S2")
            q = ph["L2"]

            def u2(g, r):
                act.wait_ge(*q.done("nm1", g))
                if q.old(g, 2):
                    act.wait_ge(*q.done("tr", g - 2))
                rows_by(ring(A_, r % 2), ring(X_, r), g, r, "u")
            pipeline(act, q.steps, [
                (4, apply_stage(q, ybank(2), scatters=True)),
                (1, u2),
                (1, copy(q, "ev", "tr", lambda r: ring(A2_, r % 2), wide(0), "y", 2)),
                (1, copy(q, "eg", "tg", lambda r: ring(A3_, r % 2), wide(6), "y", 2)),
                (0, root(q, "sq1", "ag1", sd1, var(mv1))),
                (3, root(q, "sq2", "ag2", sd2, var(mv2)))])
            finish(act, "L2")
            gated("C2")
            sums("S3")
            gated("L3")


_INS = ["x", "src", "dst", "edge_type_9", "L0_gnn_W", "L0_gnn_gamma", "L0_gnn_beta", "L1_gnn_W", "L1_gnn_attn_w",
        "L2_gnn_gamma", "L2_gnn_beta", "L2_gnn_W_self", "L2_gnn_W_neigh", "L2_gnn_b", "L3_gnn_W_msg", "L3_gnn_b_msg",
        "L3_gnn_edge_embed", "L3_gnn_W_ih", "L3_gnn_W_hh", "L3_gnn_b_ih", "L3_gnn_b_hh"]


def kernel(**inputs):
    import numpy as _np
    import concourse.bacc as _bacc
    from concourse import mybir as _mybir
    from concourse.bass_utils import run_bass_kernel_spmd as _run
    nc = _bacc.Bacc("TRN2", target_bir_lowering=False, num_devices=1)
    arrays, args = {}, []
    for name in _INS:
        a = _np.ascontiguousarray(inputs[name])
        arrays[f"in_{name}_dram"] = a
        args.append(nc.dram_tensor(f"in_{name}_dram", a.shape, _mybir.dt.from_np(a.dtype), kind="ExternalInput").ap())
    shape = inputs["x"].shape
    args.append(nc.dram_tensor("out_0_dram", shape, _mybir.dt.float32, kind="ExternalOutput").ap())
    gnn_program(nc, *args)
    r = _run(nc, [arrays], core_ids=[0])
    return r.results[0]["out_0_dram"]
```
